# Optimizing a Trainium2 kernel written in Bass

```python
import numpy as np
import jax
import jax.numpy as jnp

def _softmax(x, axis=-1):
    return jax.nn.softmax(x, axis=axis)
def _gelu(x):
    return jax.nn.gelu(x, approximate=True)
def _silu(x):
    return jax.nn.silu(x)
def _sigmoid(x):
    return jax.nn.sigmoid(x)
def _layernorm(x, axis=-1, eps=1e-5):
    m = jnp.mean(x, axis=axis, keepdims=True)
    v = jnp.var(x, axis=axis, keepdims=True)
    return (x - m) / jnp.sqrt(v + eps)
def _scatter_add(tgt, idx, src, axis=0):
    return tgt.at[idx].add(src)
def _segment_sum(src, seg, n):
    return jax.ops.segment_sum(src, seg, n)

kernel_name = 'mk_adj_ffn_d1_adj_256_d0467a'

def setup_inputs(seed: int = 0):
    np.random.seed(seed)
    _w = jnp.asarray
    def _rec_inputs():
        import jax
        import jax.numpy as jnp
        _gk = jax.random.key(seed)
        x = -0.0005207 + 1.001 * jax.random.normal(jax.random.fold_in(_gk, 1), (3327, 256), jnp.float32)
        _w = (1.0 + jnp.arange(3327, dtype=jnp.float32)) ** -0.5
        _w = _w / _w.mean()
        _pij = jnp.clip(0.00240457 * _w[:, None] * _w[None, :], 0.0, 1.0)
        _a = jax.random.uniform(jax.random.fold_in(_gk, 2), (3327, 3327)) < _pij
        _a = jnp.logical_or(_a, jnp.eye(3327, dtype=bool))
        _af = _a.astype(jnp.float32)
        _af = _af * jax.random.uniform(jax.random.fold_in(_gk, 3), (3327, 3327), jnp.float32, 0.05, 1)
        adj = _af
        return x, adj
    x, adj = _rec_inputs()
    def _L0_gnn_setup():
        import jax, jax.numpy as jnp
        import numpy as np
        D_IN = 256
        D_ATTN = 64
        STEPS = 2
        TOP_P = 0.9
        TAU = 1.0
        LN_EPS = 1e-05
        N_NODES = 8192

        def _top_p_attention(X, W1, W2, W3):
            q = X @ W1.T @ W2.T
            k = X @ W3.T
            logits = q @ k.T / TAU
            probs = jax.nn.softmax(logits, axis=-1)
            idx = jnp.argsort(-probs, axis=-1)
            sp = jnp.take_along_axis(probs, idx, axis=-1)
            cs = jnp.cumsum(sp, axis=-1)
            keep_sorted = cs - sp < TOP_P
            rows = jnp.arange(probs.shape[0])[:, None]
            mask = jnp.zeros(probs.shape, dtype=bool).at[rows, idx].set(keep_sorted)
            A = probs * mask
            return A / jnp.maximum(A.sum(-1, keepdims=True), 1e-12)
        key = jax.random.key(seed)
        ks = jax.random.split(key, 8)
        N, d, da, steps = (N_NODES, D_IN, D_ATTN, STEPS)
        X = jax.random.normal(ks[0], (N, d), dtype=jnp.float32)
        S = jax.random.uniform(ks[1], (N, N), dtype=jnp.float32)
        W1 = jax.random.normal(ks[2], (da, d), dtype=jnp.float32) / np.sqrt(d)
        W2 = jax.random.normal(ks[3], (da, da), dtype=jnp.float32) / np.sqrt(da)
        W3 = jax.random.normal(ks[4], (da, d), dtype=jnp.float32) / np.sqrt(d)
        U1 = jax.random.normal(ks[5], (steps, d, d), dtype=jnp.float32) / np.sqrt(d)
        U2 = jax.random.normal(ks[6], (steps, d, d), dtype=jnp.float32) / np.sqrt(d)
        ln_g = jnp.ones((d,), dtype=jnp.float32)
        ln_b = jnp.zeros((d,), dtype=jnp.float32)
        return {'X': X, 'S': S, 'W1': W1, 'W2': W2, 'W3': W3, 'U1': U1, 'U2': U2, 'ln_g': ln_g, 'ln_b': ln_b}
    _L0_gnn_all = _L0_gnn_setup()
    _L0_gnn_in = {k: v for k, v in _L0_gnn_all.items() if k in ('W1', 'W2', 'W3', 'U1', 'U2', 'ln_g', 'ln_b', )}
    del _L0_gnn_all

    def _L0_ffn_setup():
        import jax, jax.numpy as jnp
        import numpy as np
        E = 8
        K = 2
        D = 256
        H = 512
        DOUT = 256
        EPS = 1e-05
        key = jax.random.key(seed)
        ks = jax.random.split(key, 9)
        s = 0.02
        return {'x': jax.random.normal(ks[0], (4, 8192, D), jnp.float32), 'gamma': 1.0 + 0.05 * jax.random.normal(ks[1], (D,), jnp.float32), 'beta': 0.05 * jax.random.normal(ks[2], (D,), jnp.float32), 'Wr': 0.01 * jax.random.normal(ks[3], (D, E), jnp.float32), 'br': jnp.zeros((E,), jnp.float32), 'W1': s * jax.random.normal(ks[4], (E, D, H), jnp.float32), 'b1': s * jax.random.normal(ks[5], (E, H), jnp.float32), 'W2': s * jax.random.normal(ks[6], (E, H, DOUT), jnp.float32), 'b2': s * jax.random.normal(ks[7], (E, DOUT), jnp.float32)}
    _L0_ffn_all = _L0_ffn_setup()
    _L0_ffn_in = {k: v for k, v in _L0_ffn_all.items() if k in ('gamma', 'beta', 'Wr', 'br', 'W1', 'b1', 'W2', 'b2', )}
    del _L0_ffn_all

    return {
        "x": x,
        "adj": adj,
        "L0_gnn_W1": _L0_gnn_in["W1"],
        "L0_gnn_W2": _L0_gnn_in["W2"],
        "L0_gnn_W3": _L0_gnn_in["W3"],
        "L0_gnn_U1": _L0_gnn_in["U1"],
        "L0_gnn_U2": _L0_gnn_in["U2"],
        "L0_gnn_ln_g": _L0_gnn_in["ln_g"],
        "L0_gnn_ln_b": _L0_gnn_in["ln_b"],
        "L0_ffn_gamma": _L0_ffn_in["gamma"],
        "L0_ffn_beta": _L0_ffn_in["beta"],
        "L0_ffn_Wr": _L0_ffn_in["Wr"],
        "L0_ffn_br": _L0_ffn_in["br"],
        "L0_ffn_W1": _L0_ffn_in["W1"],
        "L0_ffn_b1": _L0_ffn_in["b1"],
        "L0_ffn_W2": _L0_ffn_in["W2"],
        "L0_ffn_b2": _L0_ffn_in["b2"],
    }

def reference(x, adj, L0_gnn_W1, L0_gnn_W2, L0_gnn_W3, L0_gnn_U1, L0_gnn_U2, L0_gnn_ln_g, L0_gnn_ln_b, L0_ffn_gamma, L0_ffn_beta, L0_ffn_Wr, L0_ffn_br, L0_ffn_W1, L0_ffn_b1, L0_ffn_W2, L0_ffn_b2):
    import jax
    import jax.numpy as jnp
    def _L0_gnn_ref(X, S, W1, W2, W3, U1, U2, ln_g, ln_b):
        import jax, jax.numpy as jnp
        import numpy as np
        D_IN = 256
        D_ATTN = 64
        STEPS = 2
        TOP_P = 0.9
        TAU = 1.0
        LN_EPS = 1e-05
        N_NODES = 8192

        def _top_p_attention(X, W1, W2, W3):
            q = X @ W1.T @ W2.T
            k = X @ W3.T
            logits = q @ k.T / TAU
            probs = jax.nn.softmax(logits, axis=-1)
            idx = jnp.argsort(-probs, axis=-1)
            sp = jnp.take_along_axis(probs, idx, axis=-1)
            cs = jnp.cumsum(sp, axis=-1)
            keep_sorted = cs - sp < TOP_P
            rows = jnp.arange(probs.shape[0])[:, None]
            mask = jnp.zeros(probs.shape, dtype=bool).at[rows, idx].set(keep_sorted)
            A = probs * mask
            return A / jnp.maximum(A.sum(-1, keepdims=True), 1e-12)
        N = X.shape[0]
        R = S + jnp.eye(N, dtype=X.dtype)
        R = R / R.sum(-1, keepdims=True)
        Z = jnp.zeros_like(X)
        Xf = X
        Xa = X
        for n in range(STEPS):
            A = _top_p_attention(Xa, W1, W2, W3)
            Xf = R @ Xf
            Xa = A @ Xa
            Z = Z + Xf @ U1[n].T + Xa @ U2[n].T
        h = X + Z
        mu = h.mean(-1, keepdims=True)
        var = jnp.mean((h - mu) ** 2, axis=-1, keepdims=True)
        return (h - mu) / jnp.sqrt(var + LN_EPS) * ln_g + ln_b

    def _L0_ffn_ref(x, gamma, beta, Wr, br, W1, b1, W2, b2):
        import jax, jax.numpy as jnp
        import numpy as np
        E = 8
        K = 2
        D = 256
        H = 512
        DOUT = 256
        EPS = 1e-05
        mu = jnp.mean(x, axis=-1, keepdims=True)
        var = jnp.mean(jnp.square(x - mu), axis=-1, keepdims=True)
        xn = (x - mu) * jax.lax.rsqrt(var + EPS) * gamma + beta
        logits = jnp.einsum('bsd,de->bse', xn, Wr) + br
        top_vals, top_idx = jax.lax.top_k(logits, K)
        w = jax.nn.softmax(top_vals, axis=-1)
        w_full = jnp.einsum('bsk,bske->bse', w, jax.nn.one_hot(top_idx, E, dtype=w.dtype))
        y = jnp.zeros(x.shape[:-1] + (DOUT,), x.dtype)
        for e in range(E):
            h = jax.nn.gelu(jnp.einsum('bsd,dh->bsh', xn, W1[e]) + b1[e], approximate=False)
            y_e = jnp.einsum('bsh,hd->bsd', h, W2[e]) + b2[e]
            y = y + y_e * w_full[..., e, None]
        return y

    x = x + _L0_gnn_ref(_layernorm(x, axis=-1), adj, L0_gnn_W1, L0_gnn_W2, L0_gnn_W3, L0_gnn_U1, L0_gnn_U2, L0_gnn_ln_g, L0_gnn_ln_b)
    x = x + _L0_ffn_ref((_layernorm(x, axis=-1))[None], L0_ffn_gamma, L0_ffn_beta, L0_ffn_Wr, L0_ffn_br, L0_ffn_W1, L0_ffn_b1, L0_ffn_W2, L0_ffn_b2)[0]
    return x


_drawn_inputs = setup_inputs


def setup_inputs(seed=0):
    import zlib

    import numpy as np

    out = dict(_drawn_inputs(seed))
    spreads = {'L0_gnn_ln_g': (1.0, 0.2), 'L0_gnn_ln_b': (0.0, 0.1), 'L0_ffn_br': (0.0, 0.1)}
    factors = {'L0_ffn_gamma': 8.0, 'L0_ffn_beta': 8.0, 'L0_ffn_b1': 21.88, 'L0_ffn_b2': 7.754}
    for name, (base, spread) in spreads.items():
        noise = np.random.default_rng([zlib.crc32(name.encode()), seed]).standard_normal(out[name].shape)
        drawn = base * np.exp(spread * noise) if base else spread * noise
        out[name] = jnp.asarray(drawn.astype(out[name].dtype))
    for name, factor in factors.items():
        out[name] = (out[name] * factor).astype(out[name].dtype)
    return out
```

```python
import concourse.bass as bass
from concourse import mybir
from contextlib import ExitStack

F32 = mybir.dt.float32
I32 = mybir.dt.int32
ALU = mybir.AluOpType
AX = mybir.AxisListType
ACT = mybir.ActivationFunctionType

P = 128
N = 3327
T = -(-N // P)
NP = T * P
LAST = N - (T - 1) * P
D = 256
DK = D // P
DA = 64
TOP_P = 0.9
EPS = 1e-5
CH = 512
CHUNKS = [(c, min(CH, NP - c)) for c in range(0, NP, CH)]
G8 = 8
NC8 = T * G8
WIN = 32
LN16 = 2.772588722239781
MAGIC = 12582912.0
HALF = T // 2
GROUPS = [(g, min(4, T - g)) for g in range(0, T, 4)]
E8 = 8
HID = 512
HC = HID // P


def loop_pairs(eng, front, back):
    front(0, 0)
    front(1, 1)
    back(0, 0)
    with eng.Fori(0, T // 2 - 1) as m:
        front(m * 2 + 2, 0)
        back(m * 2 + 1, 1)
        front(m * 2 + 3, 1)
        back(m * 2 + 2, 0)
    back(T - 1, 1)


def build(nc, a, out):
    ctx = ExitStack()
    with ctx:
        gnn = ctx.enter_context(ExitStack())

        def sb(name, shape, dt=F32):
            return gnn.enter_context(nc.sbuf_tensor(name, shape, dt))

        def sb2(name, shape, dt=F32):
            return ctx.enter_context(nc.sbuf_tensor(name, shape, dt))

        def pb(name, cols=512):
            return ctx.enter_context(nc.psum_tensor(name, [P, cols], F32))

        def sem(name):
            return ctx.enter_context(nc.semaphore(name))

        h_dram = nc.dram_tensor("h_dram", (P, T, D), F32, kind="Internal").ap()
        X0 = sb("X0", [P, T, D + 1])
        Xf1 = sb("Xf1", [P, T, D + 1])
        Xa1 = sb("Xa1", [P, T, D])
        QK = sb("QK", [P, NP])
        QKn = sb("QKn", [P, NP])
        ident = sb("ident", [P, P])
        WqkT = sb("WqkT", [P, DK, P])
        W1 = sb("W1", [DA, D])
        W2T = sb("W2T", [DA, DA])
        U1T = sb("U1T", [P, 2, DK, D])
        U2T = sb("U2T", [P, 2, DK, D])
        qw = sb("qw", [DA, 2, P])
        xw = sb("xw", [P, 2, 2, D])
        xT = sb("xT", [P, 4, P])
        hb = sb("hb", [P, 2, D])
        stat = sb("stat", [P, T, 6])
        mv = sb("mv", [P, T, 2])
        rstd = sb("rstd", [P, T])

        banks = [pb(f"bank{i}") for i in range(8)]
        psL = banks[0:2]
        psT = banks[2:4]
        psR = banks[4:6]
        psA = banks[6]
        psM = banks[7]

        x_in, w_in, st_ok, sq_ok, id0, id1 = (sem(n) for n in ("x_in", "w_in", "st_ok", "sq_ok", "id0", "id1"))
        wq_ps, wq_ok, xn_ok, xt_ps, xt_ok, qk_ps, qk_ok, c1 = (sem(n) for n in (
            "wq_ps", "wq_ok", "xn_ok", "xt_ps", "xt_ok", "qk_ps", "qk_ok", "c1"))
        xall = Xf1[:, :, 0:D]
        with nc.Block() as block:
            @block.sync
            def _(sp):
                sp.dma_start(xall, a["x"].rearrange("(t p) d -> p t d", p=P)).then_inc(x_in, 16)
                sp.dma_start(W1[:, :], a["W1"]).then_inc(w_in, 16)
                sp.dma_start(W2T[:, :], a["W2T"]).then_inc(w_in, 16)
                sp.dma_start(WqkT[:, :, 0:DA], a["W3T"].rearrange("(k p) n -> p k n", p=P)).then_inc(w_in, 16)
                sp.dma_start(U1T[:, :, :, :], a["U1T"].rearrange("s (k p) n -> p s k n", p=P)).then_inc(w_in, 16)
                sp.dma_start(U2T[:, :, :, :], a["U2T"].rearrange("s (k p) n -> p s k n", p=P)).then_inc(w_in, 16)
                sp.wait_ge(w_in, 80)

            @block.gpsimd
            def _(pool):
                pool.memset(ident[:, :], 0.0).then_inc(id0, 1)
                pool.wait_ge(id0, 1)
                pool.affine_select(out=ident[:, :], in_=ident[:, :], compare_op=ALU.not_equal, fill=1.0,
                                   base=0, pattern=[[-1, P]], channel_multiplier=1).then_inc(id1, 1)

            @block.vector
            def _(dve):
                dve.memset(X0[:, :, D:D + 1], 1.0)
                dve.wait_ge(x_in, 16)
                for t in range(T):
                    last = dve.bn_stats(stat[:, t, :], xall[:, t, :])
                last.then_inc(c1, 1)
                dve.wait_ge(c1, 1)
                for t in range(T):
                    last = dve.bn_aggr(mv[:, t, :], stat[:, t, :])
                last.then_inc(c1, 1)
                dve.wait_ge(c1, 2)
                dve.tensor_scalar(rstd[:, :], mv[:, :, 1], EPS, None, ALU.add).then_inc(st_ok, 1)
                dve.wait_ge(sq_ok, 1)
                dve.reciprocal(rstd[:, :], rstd[:, :]).then_inc(c1, 1)
                dve.wait_ge(wq_ps, 1)
                dve.tensor_copy(WqkT[:, :, DA:P], psM[:, 0:P].rearrange("p (k n) -> p k n", k=DK)).then_inc(wq_ok, 1)
                dve.wait_ge(c1, 3)
                for t in range(T):
                    dve.tensor_scalar(X0[:, t, 0:D], xall[:, t, :], mv[:, t, 0:1], rstd[:, t:t + 1],
                                      ALU.subtract, ALU.mult).then_inc(xn_ok, 1)
                dve.wait_ge(xn_ok, T)
                dve.memset(Xf1[:, :, D:D + 1], 1.0)

            @block.scalar
            def _(act):
                act.wait_ge(st_ok, 1)
                act.activation(rstd[:, :], rstd[:, :], ACT.Sqrt).then_inc(sq_ok, 1)
                for t in range(T):
                    act.wait_ge(xt_ps, t + 1)
                    if t >= 1:
                        act.wait_ge(qk_ps, t)
                    act.copy(xT[:, 0:DK, :], psT[t % 2][:, 0:D].rearrange("p (k n) -> p k n", k=DK)).then_inc(xt_ok, 1)
                    act.wait_ge(qk_ps, t + 1)
                    act.copy(QK[:, t * P:(t + 1) * P], psL[t % 2][:, 0:P]).then_inc(qk_ok, 1)

            @block.tensor
            def _(pe):
                pe.wait_ge(w_in, 80)
                for k in range(DK):
                    last = pe.matmul(psM[:, k * DA:(k + 1) * DA], W1[:, k * P:(k + 1) * P], W2T[:, :],
                                     start=True, stop=True)
                last.then_inc(wq_ps, 1)
                pe.wait_ge(id1, 1)
                pe.wait_ge(wq_ok, 1)
                for t in range(T):
                    pe.wait_ge(xn_ok, t + 1)
                    if t >= 2:
                        pe.wait_ge(xt_ok, t - 1)
                    for k in range(DK):
                        last = pe.transpose(psT[t % 2][:, k * P:(k + 1) * P], X0[:, t, k * P:(k + 1) * P], ident[:, :])
                    last.then_inc(xt_ps, 1)
                    pe.wait_ge(xt_ok, t + 1)
                    if t >= 2:
                        pe.wait_ge(qk_ok, t - 1)
                    for k in range(DK):
                        last = pe.matmul(psL[t % 2][:, 0:P], WqkT[:, k, :], xT[:, k, :], start=(k == 0), stop=(k == DK - 1))
                    last.then_inc(qk_ps, 1)

        L = sb("L", [P, NP])
        E = sb("E", [P, 2, NP])
        M = sb("M", [P, NP])
        adj = sb("adj", [P, 2, HALF, P])
        AT = sb("AT", [P, 2, 4, P])
        CL = sb("CL", [P, 2, NC8])
        CE = sb("CE", [P, 2, NC8])
        U = sb("U", [P, WIN])
        cum = sb("cum", [P, WIN])
        wv = sb("wv", [P, WIN])
        ones = sb("ones", [P, WIN])
        nm = sb("nm", [P, 2])
        S = sb("S", [P, 2])
        st = sb("st", [P, 4])
        new = sb("new", [P, 4])
        und = sb("und", [P, 4], I32)
        hiF = sb("hiF", [P, 2])
        tF = sb("tF", [P, 2])
        lo = sb("lo", [P, 1])
        sm = sb("sm", [P, 16])
        gei = sb("gei", [P, 2], I32)
        fl = sb("fl", [P, 32])
        flT = sb("flT", [P, 32])
        fr = sb("fr", [P, 1])
        fg = sb("fg", [1, 4])
        open_i = sb("open_i", [1, 1], I32)
        sinv = sb("sinv", [P, 2])
        rinv = sb("rinv", [P, 1])
        hx = sb("hx", [P, 2, D])

        def step(s):
            Xf, Xa = (X0, X0) if s == 0 else (Xf1, Xa1)
            qk = QK if s == 0 else QKn
            adj_in = [sem(f"adj_in{h}_{s}") for h in range(2)]
            hx_in = [sem(f"hx_in{h}_{s}") for h in range(2)]
            (adj_used, qw_ok, lg_ps, lg_ev, cl_ok, e_ok, a_ok, t_ps,
             t_ev, at_used, xw_ok, xt_ps, xt_ok, z_ps, h_ok, h_out, qn_ok, ch) = (
                sem(f"{name}_{s}") for name in (
                    "adj_used", "qw_ok", "lg_ps", "lg_ev", "cl_ok", "e_ok", "a_ok", "t_ps",
                    "t_ev", "at_used", "xw_ok", "xt_ps", "xt_ok", "z_ps", "h_ok", "h_out", "qn_ok", "ch"))
            NCH = len(CHUNKS)
            NG = len(GROUPS)
            with nc.Block() as block:
                @block.sync
                def _(sp):
                    for h in range(2):
                        sp.dma_start(adj[:, h, :, :], a["adjT"][0, :, h * HALF:(h + 1) * HALF, :]).then_inc(adj_in[h], 16)
                    with sp.Fori(1, T) as i:
                        for h in range(2):
                            free = sp.snap(i * 2 - 1 + h)
                            src = a["adjT"][bass.ds(i, 1), :, h * HALF:(h + 1) * HALF, :]
                            sp.wait_ge(adj_used, free)
                            sp.dma_start(adj[:, h, :, :], src.rearrange("a p j n -> p (a j) n")).then_inc(adj_in[h], 16)

                @block.gpsimd
                def _(pool):
                    def put(i, p):
                        dst = h_dram[:, bass.ds(i, 1), :]
                        pool.wait_ge(h_ok, i + 1)
                        pool.dma_start(dst, hb[:, p:p + 1, :]).then_inc(h_out, 16)
                    if s == 0:
                        with pool.Fori(0, T // 2) as m:
                            put(m * 2, 0)
                            put(m * 2 + 1, 1)
                    else:
                        for p in range(2):
                            pool.dma_start(hx[:, p:p + 1, :], h_dram[:, p:p + 1, :]).then_inc(hx_in[p], 16)
                        with pool.Fori(0, T // 2 - 1) as m:
                            for p in range(2):
                                put(m * 2 + p, p)
                                pool.dma_start(hx[:, p:p + 1, :], h_dram[:, bass.ds(m * 2 + 2 + p, 1), :]).then_inc(hx_in[p], 16)
                        put(T - 2, 0)
                        put(T - 1, 1)
                    pool.wait_ge(h_out, 16 * T)

                @block.tensor
                def _(pe):
                    def front(i, p):
                        pe.wait_ge(qw_ok, i + 1)
                        for c, (c0, w) in enumerate(CHUNKS):
                            if not isinstance(i, int):
                                pe.wait_ge(lg_ev, i * NCH + c - 1)
                            elif i * NCH + c - 1 > 0:
                                pe.wait_ge(lg_ev, i * NCH + c - 1)
                            pe.matmul(psL[(i_par(p) * NCH + c) % 2][:, 0:w], qw[:, p, :], qk[0:DA, c0:c0 + w],
                                      start=True, stop=True).then_inc(lg_ps, 1)
                        if not isinstance(i, int) or i >= 2:
                            pe.wait_ge(xw_ok, i - 1)
                        for h in range(2):
                            pe.wait_ge(adj_in[h], i * 16 + 16)
                            for j in range(HALF):
                                jt = h * HALF + j
                                last = pe.matmul(psR[p][:, 0:D + 1], adj[:, h, j, :], Xf[:, jt, :],
                                                 start=(jt == 0), stop=(jt == T - 1))
                            last.then_inc(adj_used, 1)

                    def turn(i, p, g):
                        g0, n = GROUPS[g]
                        if not isinstance(i, int) or i * NG + g - 1 > 0:
                            pe.wait_ge(t_ev, i * NG + g - 1)
                        for y in range(n):
                            last = pe.transpose(psT[(i_par(p) * NG + g) % 2][:, y * P:(y + 1) * P],
                                                E[:, p, (g0 + y) * P:(g0 + y + 1) * P], ident[:, :])
                        last.then_inc(t_ps, 1)

                    def back(i, p):
                        pe.wait_ge(a_ok, i + 1)
                        turn(i, p, 0)
                        for g, (g0, n) in enumerate(GROUPS):
                            if g + 1 < NG:
                                turn(i, p, g + 1)
                            if g + 2 == NG:
                                last_turn = True
                            pe.wait_ge(t_ev, i * NG + g + 1)
                            if g == 0 and (not isinstance(i, int) or i >= 1):
                                pe.wait_ge(h_ok, i)
                            for y in range(n):
                                jt = g0 + y
                                last = pe.matmul(psA[:, 0:D], AT[:, (i_par(p) * NG + g) % 2, y, :], Xa[:, jt, 0:D],
                                                 start=(jt == 0), stop=(jt == T - 1))
                            last.then_inc(at_used, 1)
                        pe.wait_ge(xw_ok, i + 1)
                        if s == 0 and (not isinstance(i, int) or i >= 1):
                            pe.wait_ge(qn_ok, i)
                        for y in range(4):
                            last = pe.transpose(psM[:, y * P:(y + 1) * P], xw[:, p, y // 2, (y % 2) * P:(y % 2 + 1) * P],
                                                ident[:, :])
                        last.then_inc(xt_ps, 1)
                        pe.wait_ge(xt_ok, i + 1)
                        for y in range(4):
                            w = U1T if y < 2 else U2T
                            last = pe.matmul(psA[:, D:2 * D], xT[:, y, :], w[:, s, y % 2, :], start=(y == 0), stop=(y == 3))
                        if s == 0:
                            for k in range(DK):
                                last = pe.matmul(psM[:, 0:P], WqkT[:, k, :], xT[:, 2 + k, :], start=(k == 0), stop=(k == 1))
                        last.then_inc(z_ps, 1)

                    loop_pairs(pe, front, back)

                @block.scalar
                def _(act):
                    def queries(i, p):
                        act.copy(qw[:, p, :], qk[DA:P, bass.ds(i * P, P)]).then_inc(qw_ok, 1)

                    def front(i, p):
                        queries(i, p)
                        for c, (c0, w) in enumerate(CHUNKS):
                            act.wait_ge(lg_ps, i * NCH + c + 1)
                            act.copy(L[:, c0:c0 + w], psL[(i_par(p) * NCH + c) % 2][:, 0:w]).then_inc(lg_ev, 1)
                        act.wait_ge(cl_ok, i + 1)
                        act.activation(CE[:, p, :], CL[:, p, :], ACT.Exp, bias=nm[:, p:p + 1])
                        if not isinstance(i, int) or i >= 2:
                            act.wait_ge(t_ps, (i - 1) * NG)
                        act.activation(E[:, p, 0:N], L[:, 0:N], ACT.Exp, bias=nm[:, p:p + 1],
                                       accum_out=S[:, p:p + 1]).then_inc(e_ok, 1)

                    def back(i, p):
                        for g, (g0, n) in enumerate(GROUPS):
                            act.wait_ge(t_ps, i * NG + g + 1)
                            if not isinstance(i, int) or i * NG + g - 1 > 0:
                                act.wait_ge(at_used, i * NG + g - 1)
                            gb = (i_par(p) * NG + g) % 2
                            act.copy(AT[:, gb, 0:n, :], psT[gb][:, 0:n * P].rearrange("p (y n) -> p y n", y=n)).then_inc(t_ev, 1)
                        act.wait_ge(xt_ps, i + 1)
                        if not isinstance(i, int) or i >= 1:
                            act.wait_ge(z_ps, i)
                        act.copy(xT[:, :, :], psM[:, :].rearrange("p (y n) -> p y n", y=4)).then_inc(xt_ok, 1)
                        if s == 0:
                            act.wait_ge(z_ps, i + 1)
                            act.copy(xq[:, p, :], psM[:, 0:P]).then_inc(qn_ok, 1)
                            act.wait_ge(qn_ok, i + 1)
                            act.copy(QKn[:, bass.ds(i * P, P)], xq[:, p, :])

                    loop_pairs(act, front, back)

                @block.vector
                def _(dve):
                    n = [0]

                    def link(ins):
                        n[0] += 1
                        ins.then_inc(ch, 1)
                        dve.wait_ge(ch, n[0])

                    def fresh():
                        dve.sem_clear(ch)
                        n[0] = 0

                    def front(i, p):
                        fresh()
                        dve.wait_ge(lg_ev, (i + 1) * NCH)
                        link(dve.memset(sm[:, 15:16], 0.0))
                        for t in range(T):
                            w = P if t < T - 1 else LAST
                            last = dve.max(CL[:, p, t * G8:(t + 1) * G8], L[:, t * P:t * P + w])
                        link(last)
                        link(dve.tensor_reduce(sm[:, 15:16], CL[:, p, :], AX.X, ALU.max))
                        dve.tensor_scalar(nm[:, p:p + 1], sm[:, 15:16], -1.0, LN16, ALU.mult, ALU.add).then_inc(cl_ok, 1)

                    def window(C, TT, Fh):
                        link(dve.tensor_reduce(sm[:, 1:2], C[:, G8 - 1:NC8:G8], AX.X, ALU.max))
                        for r in range(WIN // G8):
                            link(dve.max(U[:, r * G8:(r + 1) * G8], C))
                            if r < WIN // G8 - 1:
                                link(dve.match_replace(C, U[:, r * G8:(r + 1) * G8], C, 0.0))
                        link(dve.tensor_tensor_scan(cum[:, :], ones[:, :], U[:, :], Fh, ALU.mult, ALU.add))
                        link(dve.scalar_tensor_tensor(wv[:, :], cum[:, :], TT, U[:, :], ALU.is_ge, ALU.mult))
                        dve.tensor_reduce(sm[:, 2:3], wv[:, :], AX.X, ALU.max)
                        link(dve.tensor_tensor(sm[:, 3:4], U[:, WIN - 1:WIN], sm[:, 1:2], ALU.max))
                        dve.tensor_tensor(new[:, 3:4], sm[:, 2:3], sm[:, 3:4], ALU.is_le)
                        link(dve.tensor_tensor(new[:, 0:1], sm[:, 2:3], sm[:, 3:4], ALU.max))
                        link(dve.scalar_tensor_tensor(wv[:, :], U[:, :], new[:, 0:1], U[:, :], ALU.is_gt, ALU.mult,
                                                      accum_out=sm[:, 4:5]))
                        link(dve.scalar_tensor_tensor(wv[:, :], U[:, :], new[:, 0:1], U[:, :], ALU.is_ge, ALU.mult,
                                                      accum_out=sm[:, 5:6]))
                        link(dve.tensor_scalar(new[:, 1:3], sm[:, 4:6], Fh, None, ALU.add))

                    def any_row(x):
                        link(dve.tensor_scalar(fl[:, 0:1], x, 0.0, None, ALU.is_gt))
                        link(dve.transpose(flT[:, :], fl[:, :]))
                        link(dve.tensor_reduce(fr[:, :], flT[:, :], AX.X, ALU.max))
                        for q in range(4):
                            last = dve.tensor_copy(fg[0:1, q:q + 1], fr[32 * q:32 * q + 1, :])
                        link(last)
                        link(dve.tensor_reduce(open_i[:, :], fg[:, :], AX.X, ALU.max))

                    def still():
                        return dve.value_load(open_i[0:1, 0:1])

                    def mass(p, t, F):
                        link(dve.scalar_tensor_tensor(M[:, :], E[:, p, :], t, E[:, p, :], ALU.is_ge, ALU.mult, accum_out=F))

                    def select(i, p):
                        TT = sm[:, 0:1]
                        fresh()
                        dve.wait_ge(e_ok, i + 1)
                        dve.tensor_scalar(lo[:, :], S[:, p:p + 1], (1 - TOP_P) * 0.9 / NP, None, ALU.mult)
                        link(dve.tensor_scalar(TT, S[:, p:p + 1], TOP_P, None, ALU.mult))
                        window(CE[:, p, :], TT, zero[:, 0:1])
                        link(dve.tensor_copy(st[:, :], new[:, :]))
                        any_row(st[:, 3:4])

                        with dve.While(still):
                            fresh()
                            link(dve.tensor_scalar(und[:, :], ones[:, 0:4], st[:, 3:4], None, ALU.mult))
                            link(dve.tensor_copy(hiF[:, 0:1], st[:, 0:1]))
                            mass(p, hiF[:, 0:1], hiF[:, 1:2])
                            dve.tensor_copy(new[:, 2:3], hiF[:, 1:2])
                            link(dve.tensor_tensor(new[:, 3:4], hiF[:, 1:2], TT, ALU.is_lt))
                            link(dve.copy_predicated(st[:, 2:4], und[:, 0:2], new[:, 2:4]))
                            link(dve.tensor_scalar(und[:, :], ones[:, 0:4], st[:, 3:4], None, ALU.mult))
                            for _ in range(2):
                                link(dve.tensor_scalar(sm[:, 6:7], hiF[:, 0:1].bitcast(I32), 0.5, None, ALU.mult))
                                link(dve.scalar_tensor_tensor(tF[:, 0:1].bitcast(I32), lo[:, :].bitcast(I32), 0.5,
                                                              sm[:, 6:7], ALU.mult, ALU.add))
                                mass(p, tF[:, 0:1], tF[:, 1:2])
                                dve.tensor_tensor(gei[:, 0:1], tF[:, 1:2], TT, ALU.is_lt)
                                dve.tensor_tensor(gei[:, 1:2], tF[:, 1:2], TT, ALU.is_lt)
                                link(dve.tensor_tensor(geo[:, :], tF[:, 1:2], TT, ALU.is_ge))
                                dve.copy_predicated(hiF[:, :], gei[:, :], tF[:, :])
                                link(dve.copy_predicated(lo[:, :], geo[:, :], tF[:, 0:1]))
                            link(dve.scalar_tensor_tensor(M[:, :], E[:, p, :], hiF[:, 0:1], E[:, p, :], ALU.is_lt, ALU.mult))
                            for t in range(T):
                                last = dve.max(CE[:, p, t * G8:(t + 1) * G8], M[:, t * P:(t + 1) * P])
                            link(last)
                            window(CE[:, p, :], TT, hiF[:, 1:2])
                            link(dve.copy_predicated(st[:, :], und[:, :], new[:, :]))
                            any_row(st[:, 3:4])
                        fresh()
                        v, Fg, Fe = st[:, 0:1], st[:, 1:2], st[:, 2:3]
                        c = lambda k: sm[:, k:k + 1]
                        link(dve.reciprocal(c(1), v))
                        link(dve.tensor_tensor(c(2), Fe, Fg, ALU.subtract))
                        link(dve.tensor_tensor(c(3), TT, Fg, ALU.subtract))
                        link(dve.tensor_tensor(c(2), c(2), c(1), ALU.mult))
                        link(dve.tensor_tensor(c(3), c(3), c(1), ALU.mult))
                        link(dve.tensor_scalar(c(2), c(2), MAGIC, -MAGIC, ALU.add, ALU.add))
                        link(dve.tensor_scalar(c(4), c(3), MAGIC, -MAGIC, ALU.add, ALU.add))
                        link(dve.tensor_scalar(c(2), c(2), 1.0, None, ALU.max))
                        link(dve.tensor_tensor(c(5), c(3), c(4), ALU.is_gt))
                        link(dve.tensor_tensor(c(4), c(4), c(5), ALU.add))
                        link(dve.scalar_tensor_tensor(c(4), c(4), 1.0, c(2), ALU.max, ALU.min))
                        link(dve.tensor_tensor(c(5), c(2), c(4), ALU.subtract))
                        link(dve.tensor_tensor(c(5), c(5), v, ALU.mult))
                        link(dve.scalar_tensor_tensor(c(8), c(4), v, Fg, ALU.mult, ALU.add))
                        link(dve.scalar_tensor_tensor(c(8), S[:, p:p + 1], 1e-12, c(8), ALU.mult, ALU.max))
                        link(dve.reciprocal(sinv[:, p:p + 1], c(8)))
                        any_row(c(5))
                        with dve.If(still()):
                            fresh()
                            link(dve.reciprocal(c(6), c(2)))
                            link(dve.tensor_tensor(c(5), c(5), c(6), ALU.mult))
                            link(dve.tensor_scalar(M[:, :], E[:, p, :], v, c(5), ALU.is_equal, ALU.mult))
                            link(dve.scalar_tensor_tensor(E[:, p, :], E[:, p, :], v, E[:, p, :], ALU.is_ge, ALU.mult))
                            dve.tensor_tensor(E[:, p, :], E[:, p, :], M[:, :], ALU.subtract).then_inc(a_ok, 1)
                        with dve.Else():
                            dve.scalar_tensor_tensor(E[:, p, :], E[:, p, :], v, E[:, p, :],
                                                     ALU.is_ge, ALU.mult).then_inc(a_ok, 1)
                        fresh()

                    def back(i, p):
                        select(i, p)
                        dve.wait_ge(adj_used, i * 2 + 2)
                        link(dve.tensor_scalar(rinv[:, :], psR[p][:, D:D + 1], 1.0, None, ALU.add))
                        link(dve.reciprocal(rinv[:, :], rinv[:, :]))
                        link(dve.tensor_tensor(xw[:, p, 0, :], psR[p][:, 0:D], Xf[:, bass.ds(i, 1), 0:D].rearrange("p a d -> p (a d)"), ALU.add))
                        link(dve.tensor_scalar(xw[:, p, 0, :], xw[:, p, 0, :], rinv[:, :], None, ALU.mult))
                        dve.wait_ge(at_used, i * NG + NG)
                        dve.tensor_scalar(xw[:, p, 1, :], psA[:, 0:D], sinv[:, p:p + 1], None, ALU.mult).then_inc(xw_ok, 1)
                        if s == 0:
                            dve.wait_ge(xw_ok, i + 1)
                            dve.tensor_copy(Xf1[:, bass.ds(i, 1), 0:D], xw[:, p, 0:1, :])
                            dve.tensor_copy(Xa1[:, bass.ds(i, 1), :], xw[:, p, 1:2, :])
                            prev = X0[:, bass.ds(i, 1), 0:D].rearrange("p a d -> p (a d)")
                        else:
                            dve.wait_ge(hx_in[p], (i - p) * 8 + 16)
                            prev = hx[:, p, :]
                        if not isinstance(i, int) or i >= 1:
                            dve.wait_ge(h_out, i * 16)
                        dve.wait_ge(z_ps, i + 1)
                        dve.tensor_tensor(hb[:, p, :], psA[:, D:2 * D], prev, ALU.add).then_inc(h_ok, 1)

                    zero = zer
                    dve.memset(zero[:, :], 0.0)
                    dve.memset(ones[:, :], 1.0)
                    dve.memset(fl[:, :], 0.0)
                    link(dve.memset(E[:, :, N:NP], 0.0))
                    loop_pairs(dve, front, back)

        def i_par(p):
            return p

        xq = sb("xq", [P, 2, P])
        zer = sb("zer", [P, 1])
        geo = sb("geo", [P, 1], I32)
        step(0)
        step(1)
        gnn.close()

        xr = sb2("xr", [P, T, D])
        xn = sb2("xn", [P, T, D])
        xnT = sb2("xnT", [P, DK, NP])
        W1e = sb2("W1e", [P, DK, E8, HID])
        W2e = sb2("W2e", [P, HC, E8, D])
        b1T = sb2("b1T", [P, E8, HC])
        b2s = sb2("b2s", [E8, D])
        vec = sb2("vec", [P, 4, D])
        wr = sb2("wr", [P, DK, E8])
        brs = sb2("brs", [P, E8])
        idn = sb2("idn", [P, P])
        stat2 = sb2("stat2", [P, T, 6])
        mv2 = sb2("mv2", [P, T, 2])
        r1 = sb2("r1", [P, T])
        r2 = sb2("r2", [P, T])
        rl = sb2("rl", [P, T, E8])
        top = sb2("top", [P, T, E8])
        wf = sb2("wf", [P, T, E8])
        den = sb2("den", [P, T])
        wT = sb2("wT", [E8, T, P])
        (f_h, f_x, f_w, f_v, f_c, f_sq, f_sqd, f_xn, f_tp, f_te, f_rp, f_rl, f_ex, f_wf, f_wtp, f_wte, f_bp, f_be, i0, i1) = (
            sem(f"f_{k}") for k in range(20))
        with nc.Block() as block:
            @block.sync
            def _(sp):
                sp.dma_start(xn[:, :, :], h_dram).then_inc(f_h, 16)
                sp.dma_start(xr[:, :, :], a["x"].rearrange("(t p) d -> p t d", p=P)).then_inc(f_x, 16)
                sp.dma_start(vec[:, :, :], a["vec"]).then_inc(f_v, 16)
                sp.dma_start(wr[:, :, :], a["Wr"].rearrange("(k p) e -> p k e", p=P)).then_inc(f_v, 16)
                sp.dma_start(brs[:, :], a["br"]).then_inc(f_v, 16)
                sp.dma_start(b2s[:, :], a["b2"]).then_inc(f_v, 16)
                sp.dma_start(b1T[:, :, :], a["b1T"]).then_inc(f_v, 16)
                sp.dma_start(W1e[:, :, :, :], a["W1e"]).then_inc(f_w, 16)
                sp.dma_start(W2e[:, :, :, :], a["W2e"]).then_inc(f_w, 16)
                sp.wait_ge(f_w, 32)

            @block.gpsimd
            def _(pool):
                pool.memset(idn[:, :], 0.0).then_inc(i0, 1)
                pool.wait_ge(i0, 1)
                pool.affine_select(out=idn[:, :], in_=idn[:, :], compare_op=ALU.not_equal, fill=1.0,
                                   base=0, pattern=[[-1, P]], channel_multiplier=1).then_inc(i1, 1)

            @block.vector
            def _(dve):
                n = [0]
                q = [0]

                def link(ins):
                    n[0] += 1
                    ins.then_inc(f_c, 1)
                    dve.wait_ge(f_c, n[0])

                def over_tiles(k):
                    return vec[:, k:k + 1, :].to_broadcast([P, T, D])

                def moments(src):
                    for t in range(T):
                        last = dve.bn_stats(stat2[:, t, :], src[:, t, :])
                    link(last)
                    for t in range(T):
                        last = dve.bn_aggr(mv2[:, t, :], stat2[:, t, :])
                    link(last)

                def rsqrt(r, var):
                    q[0] += 1
                    dve.tensor_scalar(r[:, :], var, EPS, None, ALU.add).then_inc(f_sq, 1)
                    dve.wait_ge(f_sqd, q[0])
                    link(dve.reciprocal(r[:, :], r[:, :]))

                def centre(dst, src, r):
                    for t in range(T):
                        last = dve.tensor_scalar(dst[:, t, :], src[:, t, :], mv2[:, t, 0:1], r[:, t:t + 1],
                                                 ALU.subtract, ALU.mult)
                    link(last)

                dve.wait_ge(f_h, 16)
                moments(xn)
                rsqrt(r1, mv2[:, :, 1])
                centre(xn, xn, r1)
                dve.wait_ge(f_v, 80)
                link(dve.tensor_tensor(xn[:, :, :], xn[:, :, :], over_tiles(0), ALU.mult))
                link(dve.tensor_tensor(xn[:, :, :], xn[:, :, :], over_tiles(1), ALU.add))
                dve.wait_ge(f_x, 16)
                link(dve.tensor_tensor(xr[:, :, :], xr[:, :, :], xn[:, :, :], ALU.add))
                moments(xr)
                rsqrt(r1, mv2[:, :, 1])
                link(dve.tensor_tensor(r2[:, :], r1[:, :], r1[:, :], ALU.mult))
                link(dve.tensor_tensor(r2[:, :], r2[:, :], mv2[:, :, 1], ALU.mult))
                rsqrt(r2, r2[:, :])
                link(dve.tensor_tensor(r1[:, :], r1[:, :], r2[:, :], ALU.mult))
                centre(xn, xr, r1)
                link(dve.tensor_tensor(xn[:, :, :], xn[:, :, :], over_tiles(2), ALU.mult))
                dve.tensor_tensor(xn[:, :, :], xn[:, :, :], over_tiles(3), ALU.add).then_inc(f_xn, 1)
                dve.wait_ge(f_rp, 1)
                link(dve.tensor_tensor(rl[:, :, :], banks[4][:, 0:T * E8].rearrange("p (t e) -> p t e", e=E8),
                                       brs[:, :].rearrange("p (a e) -> p a e", a=1).to_broadcast([P, T, E8]), ALU.add))
                for t in range(T):
                    last = dve.max(top[:, t, :], rl[:, t, :])
                link(last)
                link(dve.tensor_tensor(wf[:, :, :], rl[:, :, :], top[:, :, 0:1].to_broadcast([P, T, E8]), ALU.subtract))
                dve.tensor_tensor(rl[:, :, :], rl[:, :, :], top[:, :, 1:2].to_broadcast([P, T, E8]), ALU.is_ge).then_inc(f_rl, 1)
                dve.wait_ge(f_rl, 1)
                dve.wait_ge(f_ex, 1)
                link(dve.tensor_tensor(wf[:, :, :], wf[:, :, :], rl[:, :, :], ALU.mult))
                link(dve.tensor_reduce(den[:, :], wf[:, :, :], AX.X, ALU.add))
                link(dve.reciprocal(den[:, :], den[:, :]))
                dve.tensor_tensor(wf[:, :, :], wf[:, :, :], den[:, :].rearrange("p (t a) -> p t a", a=1).to_broadcast([P, T, E8]),
                                  ALU.mult).then_inc(f_wf, 1)
                for t in range(T):
                    dve.wait_ge(f_bp, t + 1)
                    dve.tensor_tensor(xr[:, t, :], banks[6 + t % 2][:, 0:D], xr[:, t, :], ALU.add).then_inc(f_be, 1)
                dve.wait_ge(f_be, T)

            @block.scalar
            def _(act):
                for k, r in enumerate((r1, r1, r2)):
                    act.wait_ge(f_sq, k + 1)
                    act.activation(r[:, :], r[:, :], ACT.Sqrt).then_inc(f_sqd, 1)
                for g in range(T // 2):
                    act.wait_ge(f_tp, g + 1)
                    act.copy(xnT[:, :, g * 2 * P:(g + 1) * 2 * P],
                             banks[g % 4][:, :].rearrange("p (k n) -> p k n", k=DK)).then_inc(f_te, 1)
                act.wait_ge(f_rl, 1)
                act.activation(wf[:, :, :], wf[:, :, :], ACT.Exp).then_inc(f_ex, 1)
                for t in range(T):
                    act.wait_ge(f_wtp, t + 1)
                    act.copy(wT[:, t, :], banks[5][0:E8, (t % 4) * P:(t % 4 + 1) * P]).then_inc(f_wte, 1)

            @block.tensor
            def _(pe):
                pe.wait_ge(i1, 1)
                pe.wait_ge(f_xn, 1)
                for g in range(T // 2):
                    if g >= 4:
                        pe.wait_ge(f_te, g - 3)
                    for k in range(DK):
                        for u in range(2):
                            last = pe.transpose(banks[g % 4][:, (k * 2 + u) * P:(k * 2 + u + 1) * P],
                                                xn[:, 2 * g + u, k * P:(k + 1) * P], idn[:, :])
                    last.then_inc(f_tp, 1)
                for t in range(T):
                    pe.wait_ge(f_te, t // 2 + 1)
                    for k in range(DK):
                        last = pe.matmul(banks[4][:, t * E8:(t + 1) * E8], xnT[:, k, t * P:(t + 1) * P], wr[:, k, :],
                                         start=(k == 0), stop=(k == DK - 1))
                last.then_inc(f_rp, 1)
                pe.wait_ge(f_wf, 1)
                for t in range(T):
                    if t >= 4:
                        pe.wait_ge(f_wte, t - 3)
                    pe.transpose(banks[5][0:E8, (t % 4) * P:(t % 4 + 1) * P], wf[:, t, :], idn[:, :]).then_inc(f_wtp, 1)
                    pe.wait_ge(f_wte, t + 1)
                    if t >= 2:
                        pe.wait_ge(f_be, t - 1)
                    pe.matmul(banks[6 + t % 2][:, 0:D], wT[:, t, :], b2s[:, :], start=True, stop=True).then_inc(f_bp, 1)

        G = sb2("G", [P, 2, HC, 2 * P])
        wfs = sb2("wfs", [P, 2, E8])
        acc = sb2("acc", [P, 2, D])
        ob = sb2("ob", [P, 1, 2, D])
        (h_psd, g_ok, y_psd, y_ok, ob_ok, o_done0, xc) = (sem(f"g_{k}") for k in range(7))
        NB = T // 2
        with nc.Block() as block:
            @block.tensor
            def _(pe):
                def up(m, e):
                    k8 = m * E8 + e
                    if not (isinstance(m, int) and e < 2):
                        pe.wait_ge(g_ok, k8 - 1)
                    for c in range(HC):
                        for k in range(DK):
                            last = pe.matmul(banks[2 * (e % 2) + c // 2][:, (c % 2) * 2 * P:(c % 2 + 1) * 2 * P],
                                             W1e[:, k, e, c * P:(c + 1) * P], xnT[:, k, bass.ds(m * 2 * P, 2 * P)],
                                             start=(k == 0), stop=(k == DK - 1))
                    last.then_inc(h_psd, 1)

                def down(m, e):
                    k8 = m * E8 + e
                    pe.wait_ge(g_ok, k8 + 1)
                    if not (isinstance(m, int) and e < 2):
                        pe.wait_ge(y_ok, k8 - 1)
                    for u in range(2):
                        for c in range(HC):
                            last = pe.matmul(banks[4 + e % 2][:, u * D:(u + 1) * D], G[:, e % 2, c, u * P:(u + 1) * P],
                                             W2e[:, c, e, :], start=(c == 0), stop=(c == HC - 1))
                    last.then_inc(y_psd, 1)

                def pair(m):
                    up(m, 0)
                    for e in range(E8):
                        if e + 1 < E8:
                            up(m, e + 1)
                        down(m, e)
                pair(0)
                with pe.Fori(1, NB) as m:
                    pair(m)

            @block.scalar
            def _(act):
                def pair(m):
                    for e in range(E8):
                        k8 = m * E8 + e
                        act.wait_ge(h_psd, k8 + 1)
                        if not (isinstance(m, int) and e < 2):
                            act.wait_ge(y_psd, k8 - 1)
                        for c in range(HC):
                            last = act.activation(G[:, e % 2, c, :], banks[2 * (e % 2) + c // 2][:, (c % 2) * 2 * P:(c % 2 + 1) * 2 * P],
                                                  ACT.Gelu, bias=b1T[:, e, c:c + 1])
                        last.then_inc(g_ok, 1)
                pair(0)
                with act.Fori(1, NB) as m:
                    pair(m)

            @block.vector
            def _(dve):
                ws = wfs

                def pair(m):
                    dve.tensor_copy(ws[:, :, :], wf[:, bass.ds(m * 2, 2), :])
                    dve.tensor_copy(acc[:, :, :], xr[:, bass.ds(m * 2, 2), :]).then_inc(xc, 1)
                    dve.wait_ge(xc, m + 1)
                    for e in range(E8):
                        k8 = m * E8 + e
                        dve.wait_ge(y_psd, k8 + 1)
                        for u in range(2):
                            dst = acc[:, u, :]
                            last = dve.scalar_tensor_tensor(dst, banks[4 + e % 2][:, u * D:(u + 1) * D], ws[:, u, e:e + 1],
                                                            acc[:, u, :], ALU.mult, ALU.add)
                            if e < E8 - 1 and u == 1:
                                last.then_inc(y_ok, 1)
                        if e < E8 - 1:
                            dve.wait_ge(y_ok, k8 + 1)
                    last.then_inc(y_ok, 1)
                    dve.wait_ge(y_ok, m * E8 + E8)
                    if not (isinstance(m, int)):
                        dve.wait_ge(o_done0, m * 16)
                    dve.tensor_copy(ob[:, 0, :, :], acc[:, :, :]).then_inc(ob_ok, 1)
                    dve.wait_ge(ob_ok, m + 1)
                pair(0)
                with dve.Fori(1, NB) as m:
                    pair(m)

            @block.sync
            def _(sp):
                with sp.Fori(0, NB - 1) as m:
                    r0 = sp.snap(m * 2 * P)
                    sp.wait_ge(ob_ok, m + 1)
                    sp.dma_start(out[bass.ds(r0, 2 * P), :].rearrange("(u p) d -> p u d", u=2), ob[:, 0, :, :]).then_inc(o_done0, 16)
                sp.wait_ge(ob_ok, NB)
                sp.dma_start(out[(NB - 1) * 2 * P:(NB - 1) * 2 * P + P, :], ob[:, 0, 0, :]).then_inc(o_done0, 16)
                sp.dma_start(out[(NB - 1) * 2 * P + P:N, :], ob[0:LAST, 0, 1, :]).then_inc(o_done0, 16)
                sp.wait_ge(o_done0, 16 * (NB + 1))


_OUT = ((N, D), "float32")


def kernel(**inputs):
    import numpy as np
    import concourse.bacc as _bacc
    from concourse import mybir as _mybir
    from concourse.bass_utils import run_bass_kernel_spmd as _run

    g = {k: np.asarray(v) for k, v in inputs.items()}
    x = np.zeros((NP, D), np.float32)
    x[:N] = g["x"]
    adjp = np.zeros((NP, NP), np.float32)
    adjp[:N, :N] = g["adj"]
    lay = {
        "x": x,
        "adjT": adjp.reshape(T, P, T, P).transpose(0, 3, 2, 1),
        "W1": g["L0_gnn_W1"],
        "W2T": g["L0_gnn_W2"].T,
        "W3T": g["L0_gnn_W3"].T,
        "U1T": g["L0_gnn_U1"].transpose(0, 2, 1),
        "U2T": g["L0_gnn_U2"].transpose(0, 2, 1),
        "vec": np.broadcast_to(np.stack([g["L0_gnn_ln_g"], g["L0_gnn_ln_b"], g["L0_ffn_gamma"], g["L0_ffn_beta"]]), (P, 4, D)),
        "Wr": g["L0_ffn_Wr"],
        "br": np.broadcast_to(g["L0_ffn_br"], (P, E8)),
        "W1e": g["L0_ffn_W1"].reshape(E8, DK, P, HID).transpose(2, 1, 0, 3),
        "W2e": g["L0_ffn_W2"].reshape(E8, HC, P, D).transpose(2, 1, 0, 3),
        "b1T": g["L0_ffn_b1"].reshape(E8, HC, P).transpose(2, 0, 1),
        "b2": g["L0_ffn_b2"],
    }
    nc = _bacc.Bacc("TRN2", target_bir_lowering=False, num_devices=1)
    arrays, aps = {}, {}
    for k, v in lay.items():
        v = np.ascontiguousarray(v)
        arrays[f"in_{k}"] = v
        aps[k] = nc.dram_tensor(f"in_{k}", v.shape, _mybir.dt.from_np(v.dtype), kind="ExternalInput").ap()
    o = nc.dram_tensor("out_0", _OUT[0], _mybir.dt.from_np(np.dtype(_OUT[1])), kind="ExternalOutput").ap()
    build(nc, aps, o)
    r = _run(nc, [arrays], core_ids=[0])
    return r.results[0]["out_0"]
```

```python
import concourse.bass as bass
from concourse import mybir
from contextlib import ExitStack

F32 = mybir.dt.float32
I32 = mybir.dt.int32
ALU = mybir.AluOpType
AX = mybir.AxisListType
ACT = mybir.ActivationFunctionType

P = 128
N = 3327
T = -(-N // P)
NP = T * P
LAST = N - (T - 1) * P
D = 256
DK = D // P
DA = 64
TOP_P = 0.9
EPS = 1e-5
CH = 512
CHUNKS = [(c, min(CH, NP - c)) for c in range(0, NP, CH)]
G8 = 8
NC8 = T * G8
WIN0 = 32
WIN = 64
HALVINGS = 3
AIM = 0.4 * WIN
LN16 = 2.772588722239781
MAGIC = 12582912.0
HALF = T // 2
GROUPS = [(g, min(4, T - g)) for g in range(0, T, 4)]
E8 = 8
HID = 512
HC = HID // P


def run_turns(eng, turn):
    for k in range(-2, 2):
        turn(k, k % 2)
    with eng.Fori(0, T // 2 - 2) as m:
        turn(m * 2 + 2, 0)
        turn(m * 2 + 3, 1)
    for k in range(T - 2, T + 2):
        turn(k, k % 2)


def there(i):
    return not isinstance(i, int) or 0 <= i < T


def reach(eng, semaphore, value):
    if not isinstance(value, int) or value > 0:
        eng.wait_ge(semaphore, value)


def build(nc, a, out):
    ctx = ExitStack()
    with ctx:
        gnn = ctx.enter_context(ExitStack())

        def sb(name, shape, dt=F32):
            return gnn.enter_context(nc.sbuf_tensor(name, shape, dt))

        def sb2(name, shape, dt=F32):
            return ctx.enter_context(nc.sbuf_tensor(name, shape, dt))

        def pb(name, cols=512):
            return ctx.enter_context(nc.psum_tensor(name, [P, cols], F32))

        def sem(name):
            return ctx.enter_context(nc.semaphore(name))

        h_dram = nc.dram_tensor("h_dram", (P, T, D), F32, kind="Internal").ap()
        X0 = sb("X0", [P, T, D + 1])
        Xf1 = sb("Xf1", [P, T, D + 1])
        Xa1 = sb("Xa1", [P, T, D])
        QK = sb("QK", [P, NP])
        QKn = sb("QKn", [P, NP])
        ident = sb("ident", [P, P])
        WqkT = sb("WqkT", [P, DK, P])
        W1 = sb("W1", [DA, D])
        W2T = sb("W2T", [DA, DA])
        U1T = sb("U1T", [P, 2, DK, D])
        U2T = sb("U2T", [P, 2, DK, D])
        qw = sb("qw", [DA, 2, P])
        xw = sb("xw", [P, 2, 2, D])
        xT = sb("xT", [P, 4, P])
        hb = sb("hb", [P, 2, D])
        stat = sb("stat", [P, T, 6])
        mv = sb("mv", [P, T, 2])
        rstd = sb("rstd", [P, T])

        banks = [pb(f"bank{i}") for i in range(8)]
        psL = banks[0:2]
        psT = banks[2:4]
        psR = banks[4:6]
        psA = banks[6]
        psM = banks[7]

        x_in, w_in, st_ok, sq_ok, id0, id1 = (sem(n) for n in ("x_in", "w_in", "st_ok", "sq_ok", "id0", "id1"))
        wq_ps, wq_ok, xn_ok, xt_ps, xt_ok, qk_ps, qk_ok, c1 = (sem(n) for n in (
            "wq_ps", "wq_ok", "xn_ok", "xt_ps", "xt_ok", "qk_ps", "qk_ok", "c1"))
        xall = Xf1[:, :, 0:D]
        with nc.Block() as block:
            @block.sync
            def _(sp):
                sp.dma_start(xall, a["x"].rearrange("(t p) d -> p t d", p=P)).then_inc(x_in, 16)
                sp.dma_start(W1[:, :], a["W1"]).then_inc(w_in, 16)
                sp.dma_start(W2T[:, :], a["W2T"]).then_inc(w_in, 16)
                sp.dma_start(WqkT[:, :, 0:DA], a["W3T"].rearrange("(k p) n -> p k n", p=P)).then_inc(w_in, 16)
                sp.dma_start(U1T[:, :, :, :], a["U1T"].rearrange("s (k p) n -> p s k n", p=P)).then_inc(w_in, 16)
                sp.dma_start(U2T[:, :, :, :], a["U2T"].rearrange("s (k p) n -> p s k n", p=P)).then_inc(w_in, 16)
                sp.wait_ge(w_in, 80)

            @block.gpsimd
            def _(pool):
                pool.memset(ident[:, :], 0.0).then_inc(id0, 1)
                pool.wait_ge(id0, 1)
                pool.affine_select(out=ident[:, :], in_=ident[:, :], compare_op=ALU.not_equal, fill=1.0,
                                   base=0, pattern=[[-1, P]], channel_multiplier=1).then_inc(id1, 1)

            @block.vector
            def _(dve):
                dve.memset(X0[:, :, D:D + 1], 1.0)
                dve.wait_ge(x_in, 16)
                for t in range(T):
                    last = dve.bn_stats(stat[:, t, :], xall[:, t, :])
                last.then_inc(c1, 1)
                dve.wait_ge(c1, 1)
                for t in range(T):
                    last = dve.bn_aggr(mv[:, t, :], stat[:, t, :])
                last.then_inc(c1, 1)
                dve.wait_ge(c1, 2)
                dve.tensor_scalar(rstd[:, :], mv[:, :, 1], EPS, None, ALU.add).then_inc(st_ok, 1)
                dve.wait_ge(sq_ok, 1)
                dve.reciprocal(rstd[:, :], rstd[:, :]).then_inc(c1, 1)
                dve.wait_ge(wq_ps, 1)
                dve.tensor_copy(WqkT[:, :, DA:P], psM[:, 0:P].rearrange("p (k n) -> p k n", k=DK)).then_inc(wq_ok, 1)
                dve.wait_ge(c1, 3)
                for t in range(T):
                    dve.tensor_scalar(X0[:, t, 0:D], xall[:, t, :], mv[:, t, 0:1], rstd[:, t:t + 1],
                                      ALU.subtract, ALU.mult).then_inc(xn_ok, 1)
                dve.wait_ge(xn_ok, T)
                dve.memset(Xf1[:, :, D:D + 1], 1.0)

            @block.scalar
            def _(act):
                act.wait_ge(st_ok, 1)
                act.activation(rstd[:, :], rstd[:, :], ACT.Sqrt).then_inc(sq_ok, 1)
                for t in range(T):
                    act.wait_ge(xt_ps, t + 1)
                    if t >= 1:
                        act.wait_ge(qk_ps, t)
                    act.copy(xT[:, 0:DK, :], psT[t % 2][:, 0:D].rearrange("p (k n) -> p k n", k=DK)).then_inc(xt_ok, 1)
                    act.wait_ge(qk_ps, t + 1)
                    act.copy(QK[:, t * P:(t + 1) * P], psL[t % 2][:, 0:P]).then_inc(qk_ok, 1)

            @block.tensor
            def _(pe):
                pe.wait_ge(w_in, 80)
                for k in range(DK):
                    last = pe.matmul(psM[:, k * DA:(k + 1) * DA], W1[:, k * P:(k + 1) * P], W2T[:, :],
                                     start=True, stop=True)
                last.then_inc(wq_ps, 1)
                pe.wait_ge(id1, 1)
                pe.wait_ge(wq_ok, 1)
                for t in range(T):
                    pe.wait_ge(xn_ok, t + 1)
                    if t >= 2:
                        pe.wait_ge(xt_ok, t - 1)
                    for k in range(DK):
                        last = pe.transpose(psT[t % 2][:, k * P:(k + 1) * P], X0[:, t, k * P:(k + 1) * P], ident[:, :])
                    last.then_inc(xt_ps, 1)
                    pe.wait_ge(xt_ok, t + 1)
                    if t >= 2:
                        pe.wait_ge(qk_ok, t - 1)
                    for k in range(DK):
                        last = pe.matmul(psL[t % 2][:, 0:P], WqkT[:, k, :], xT[:, k, :], start=(k == 0), stop=(k == DK - 1))
                    last.then_inc(qk_ps, 1)

        L = sb("L", [P, NP])
        E = sb("E", [P, 2, NP])
        M = sb("M", [P, NP])
        adj = sb("adj", [P, 2, HALF, P])
        AT = sb("AT", [P, 2, 4, P])
        CL = sb("CL", [P, 2, NC8])
        CE = sb("CE", [P, 2, NC8])
        U = sb("U", [P, WIN])
        cum = sb("cum", [P, WIN])
        wv = sb("wv", [P, WIN])
        ones = sb("ones", [P, WIN])
        nm = sb("nm", [P, 2])
        S = sb("S", [P, 2])
        st = sb("st", [P, 4])
        new = sb("new", [P, 4])
        und = sb("und", [P, 4], I32)
        hiF = sb("hiF", [P, 2])
        tF = sb("tF", [P, 2])
        loF = sb("loF", [P, 2])
        sm = sb("sm", [P, 16])
        gei = sb("gei", [P, 2], I32)
        fl = sb("fl", [P, 32])
        flT = sb("flT", [P, 32])
        fr = sb("fr", [P, 1])
        fg = sb("fg", [1, 4])
        open_i = sb("open_i", [1, 1], I32)
        sinv = sb("sinv", [P, 2])
        rinv = sb("rinv", [P, 1])
        hx = sb("hx", [P, 2, D])

        def step(s):
            Xf, Xa = (X0, X0) if s == 0 else (Xf1, Xa1)
            qk = QK if s == 0 else QKn
            adj_in = [sem(f"adj_in{h}_{s}") for h in range(2)]
            hx_in = [sem(f"hx_in{h}_{s}") for h in range(2)]
            (adj_used, qw_ok, lg_ps, lg_ev, cl_ok, e_ok, a_ok, t_ps,
             t_ev, at_used, xw_ok, xt_ps, xt_ok, z_ps, h_ok, h_out, ce_ok, ch) = (
                sem(f"{name}_{s}") for name in (
                    "adj_used", "qw_ok", "lg_ps", "lg_ev", "cl_ok", "e_ok", "a_ok", "t_ps",
                    "t_ev", "at_used", "xw_ok", "xt_ps", "xt_ok", "z_ps", "h_ok", "h_out", "ce_ok", "ch"))
            NCH = len(CHUNKS)
            NG = len(GROUPS)
            with nc.Block() as block:
                @block.sync
                def _(sp):
                    for h in range(2):
                        sp.dma_start(adj[:, h, :, :], a["adjT"][0, :, h * HALF:(h + 1) * HALF, :]).then_inc(adj_in[h], 16)
                    with sp.Fori(1, T) as i:
                        for h in range(2):
                            free = sp.snap(i * 2 - 1 + h)
                            src = a["adjT"][bass.ds(i, 1), :, h * HALF:(h + 1) * HALF, :]
                            sp.wait_ge(adj_used, free)
                            sp.dma_start(adj[:, h, :, :], src.rearrange("a p j n -> p (a j) n")).then_inc(adj_in[h], 16)

                @block.gpsimd
                def _(pool):
                    def put(i, p):
                        dst = h_dram[:, bass.ds(i, 1), :]
                        pool.wait_ge(h_ok, i + 1)
                        pool.dma_start(dst, hb[:, p:p + 1, :]).then_inc(h_out, 16)
                    if s == 0:
                        with pool.Fori(0, T // 2) as m:
                            put(m * 2, 0)
                            put(m * 2 + 1, 1)
                    else:
                        for p in range(2):
                            pool.dma_start(hx[:, p:p + 1, :], h_dram[:, p:p + 1, :]).then_inc(hx_in[p], 16)
                        with pool.Fori(0, T // 2 - 1) as m:
                            for p in range(2):
                                put(m * 2 + p, p)
                                pool.dma_start(hx[:, p:p + 1, :], h_dram[:, bass.ds(m * 2 + 2 + p, 1), :]).then_inc(hx_in[p], 16)
                        put(T - 2, 0)
                        put(T - 1, 1)
                    pool.wait_ge(h_out, 16 * T)

                @block.tensor
                def _(pe):
                    def turned(i, p, g):
                        g0, n = GROUPS[g]
                        reach(pe, t_ev, i * NG + g - 1)
                        for y in range(n):
                            last = pe.transpose(psT[(p * NG + g) % 2][:, y * P:(y + 1) * P],
                                                E[:, p, (g0 + y) * P:(g0 + y + 1) * P], ident[:, :])
                        last.then_inc(t_ps, 1)

                    def attend(i, p, between):
                        pe.wait_ge(a_ok, i + 1)
                        turned(i, p, 0)
                        for g, (g0, n) in enumerate(GROUPS):
                            if g + 1 < NG:
                                turned(i, p, g + 1)
                            if g == 1:
                                between()
                            pe.wait_ge(t_ev, i * NG + g + 1)
                            if g == 0:
                                reach(pe, xw_ok, i)
                            for y in range(n):
                                jt = g0 + y
                                last = pe.matmul(psA[:, 0:D], AT[:, (p * NG + g) % 2, y, :], Xa[:, jt, 0:D],
                                                 start=(jt == 0), stop=(jt == T - 1))
                            last.then_inc(at_used, 1)

                    def post_turn(i, p):
                        pe.wait_ge(xw_ok, i + 1)
                        reach(pe, h_ok, i)
                        for y in range(4):
                            last = pe.transpose(psM[:, y * P:(y + 1) * P], xw[:, p, y // 2, (y % 2) * P:(y % 2 + 1) * P],
                                                ident[:, :])
                        last.then_inc(xt_ps, 1)

                    def post_products(i):
                        pe.wait_ge(xt_ok, i + 1)
                        for y in range(4):
                            w = U1T if y < 2 else U2T
                            last = pe.matmul(psM[:, 0:D], xT[:, y, :], w[:, s, y % 2, :], start=(y == 0), stop=(y == 3))
                        if s == 0:
                            for k in range(DK):
                                last = pe.matmul(psM[:, D:D + P], WqkT[:, k, :], xT[:, 2 + k, :], start=(k == 0), stop=(k == 1))
                        last.then_inc(z_ps, 1)

                    def diffuse(i, p):
                        reach(pe, xw_ok, i - 1)
                        for h in range(2):
                            pe.wait_ge(adj_in[h], i * 16 + 16)
                            for j in range(HALF):
                                jt = h * HALF + j
                                last = pe.matmul(psR[p][:, 0:D + 1], adj[:, h, j, :], Xf[:, jt, :],
                                                 start=(jt == 0), stop=(jt == T - 1))
                            last.then_inc(adj_used, 1)

                    def logits(i, p):
                        pe.wait_ge(qw_ok, i + 1)
                        for c, (c0, w) in enumerate(CHUNKS):
                            reach(pe, lg_ev, i * NCH + c - 1)
                            pe.matmul(psL[(p * NCH + c) % 2][:, 0:w], qw[:, p, :], qk[0:DA, c0:c0 + w],
                                      start=True, stop=True).then_inc(lg_ps, 1)

                    def turn(k, p):
                        if there(k - 2):
                            post_turn(k - 2, p)
                        if there(k - 1):
                            attend(k - 1, 1 - p, lambda: post_products(k - 2) if there(k - 2) else None)
                        elif there(k - 2):
                            post_products(k - 2)
                        if there(k):
                            diffuse(k, p)
                        if there(k + 2):
                            logits(k + 2, p)

                    run_turns(pe, turn)

                @block.scalar
                def _(act):
                    def candidates(i, p):
                        act.wait_ge(cl_ok, i + 1)
                        act.activation(CE[:, p, :], CL[:, p, :], ACT.Exp, bias=nm[:, p:p + 1]).then_inc(ce_ok, 1)

                    def exponentials(i, p):
                        reach(act, t_ps, (i - 1) * NG)
                        act.activation(E[:, p, 0:N], L[:, 0:N], ACT.Exp, bias=nm[:, p:p + 1],
                                       accum_out=S[:, p:p + 1]).then_inc(e_ok, 1)

                    def take_logits(i, p):
                        act.copy(qw[:, p, :], qk[DA:P, bass.ds(i * P, P)]).then_inc(qw_ok, 1)
                        if there(i - 1):
                            act.wait_ge(e_ok, i)
                        for c, (c0, w) in enumerate(CHUNKS):
                            act.wait_ge(lg_ps, i * NCH + c + 1)
                            act.copy(L[:, c0:c0 + w], psL[(p * NCH + c) % 2][:, 0:w]).then_inc(lg_ev, 1)

                    def take_turned(i, p, g):
                        g0, n = GROUPS[g]
                        gb = (p * NG + g) % 2
                        act.wait_ge(t_ps, i * NG + g + 1)
                        reach(act, at_used, i * NG + g - 1)
                        act.copy(AT[:, gb, 0:n, :], psT[gb][:, 0:n * P].rearrange("p (y n) -> p y n", y=n)).then_inc(t_ev, 1)

                    def take_rows(i):
                        act.wait_ge(xt_ps, i + 1)
                        reach(act, z_ps, i)
                        act.copy(xT[:, :, :], psM[:, :].rearrange("p (y n) -> p y n", y=4)).then_inc(xt_ok, 1)

                    def turn(k, p):
                        if there(k - 2):
                            take_rows(k - 2)
                        if there(k - 1):
                            for g in range(NG):
                                take_turned(k - 1, 1 - p, g)
                        if there(k + 1):
                            candidates(k + 1, 1 - p)
                            exponentials(k + 1, 1 - p)
                        if there(k + 2):
                            take_logits(k + 2, p)

                    run_turns(act, turn)

                @block.vector
                def _(dve):
                    n = [0]

                    def link(ins):
                        n[0] += 1
                        ins.then_inc(ch, 1)
                        dve.wait_ge(ch, n[0])

                    def fresh():
                        dve.sem_clear(ch)
                        n[0] = 0

                    c = lambda k: sm[:, k:k + 1]

                    def largest(i, p):
                        fresh()
                        dve.wait_ge(lg_ev, (i + 1) * NCH)
                        link(dve.memset(c(15), 0.0))
                        for t in range(T):
                            w = P if t < T - 1 else LAST
                            last = dve.max(CL[:, p, t * G8:(t + 1) * G8], L[:, t * P:t * P + w])
                        link(last)
                        link(dve.tensor_reduce(c(15), CL[:, p, :], AX.X, ALU.max))
                        dve.tensor_scalar(nm[:, p:p + 1], c(15), -1.0, LN16, ALU.mult, ALU.add).then_inc(cl_ok, 1)

                    def window(C, W, TT, Fh):
                        link(dve.tensor_reduce(c(1), C[:, G8 - 1:NC8:G8], AX.X, ALU.max))
                        for r in range(W // G8):
                            link(dve.max(U[:, r * G8:(r + 1) * G8], C))
                            if r < W // G8 - 1:
                                link(dve.match_replace(C, U[:, r * G8:(r + 1) * G8], C, 0.0))
                        link(dve.tensor_tensor_scan(cum[:, 0:W], ones[:, 0:W], U[:, 0:W], Fh, ALU.mult, ALU.add))
                        link(dve.scalar_tensor_tensor(wv[:, 0:W], cum[:, 0:W], TT, U[:, 0:W], ALU.is_ge, ALU.mult))
                        dve.tensor_reduce(c(2), wv[:, 0:W], AX.X, ALU.max)
                        link(dve.tensor_tensor(c(3), U[:, W - 1:W], c(1), ALU.max))
                        dve.tensor_tensor(new[:, 3:4], c(2), c(3), ALU.is_le)
                        link(dve.tensor_tensor(new[:, 0:1], c(2), c(3), ALU.max))
                        link(dve.scalar_tensor_tensor(wv[:, 0:W], U[:, 0:W], new[:, 0:1], U[:, 0:W], ALU.is_gt, ALU.mult,
                                                      accum_out=c(4)))
                        link(dve.scalar_tensor_tensor(wv[:, 0:W], U[:, 0:W], new[:, 0:1], U[:, 0:W], ALU.is_ge, ALU.mult,
                                                      accum_out=c(5)))
                        link(dve.tensor_scalar(new[:, 1:3], sm[:, 4:6], Fh, None, ALU.add))

                    def any_row(x):
                        link(dve.tensor_scalar(fl[:, 0:1], x, 0.0, None, ALU.is_gt))
                        link(dve.transpose(flT[:, :], fl[:, :]))
                        link(dve.tensor_reduce(fr[:, :], flT[:, :], AX.X, ALU.max))
                        for q in range(4):
                            last = dve.tensor_copy(fg[0:1, q:q + 1], fr[32 * q:32 * q + 1, :])
                        link(last)
                        link(dve.tensor_reduce(open_i[:, :], fg[:, :], AX.X, ALU.max))

                    def still():
                        return dve.value_load(open_i[0:1, 0:1])

                    def bracket(TT):
                        dve.tensor_tensor(gei[:, 0:1], tF[:, 1:2], TT, ALU.is_lt)
                        dve.tensor_tensor(gei[:, 1:2], tF[:, 1:2], TT, ALU.is_lt)
                        dve.tensor_tensor(geo[:, 0:1], tF[:, 1:2], TT, ALU.is_ge)
                        link(dve.tensor_tensor(geo[:, 1:2], tF[:, 1:2], TT, ALU.is_ge))
                        dve.copy_predicated(hiF[:, :], gei[:, :], tF[:, :])
                        link(dve.copy_predicated(loF[:, :], geo[:, :], tF[:, :]))

                    def select(i, p):
                        TT = c(0)
                        fresh()
                        dve.wait_ge(e_ok, i + 1)
                        dve.tensor_scalar(loF[:, 0:1], S[:, p:p + 1], (1 - TOP_P) * 0.9 / NP, None, ALU.mult)
                        dve.tensor_scalar(loF[:, 1:2], S[:, p:p + 1], 0.95, None, ALU.mult)
                        link(dve.tensor_scalar(TT, S[:, p:p + 1], TOP_P, None, ALU.mult))
                        window(CE[:, p, :], WIN0, TT, zer[:, 0:1])
                        dve.tensor_copy(hiF[:, 0:1], new[:, 0:1])
                        dve.tensor_copy(hiF[:, 1:2], new[:, 2:3])
                        link(dve.tensor_copy(st[:, :], new[:, :]))
                        any_row(st[:, 3:4])

                        with dve.While(still):
                            fresh()
                            for _ in range(HALVINGS):
                                link(dve.tensor_scalar(c(6), hiF[:, 0:1].bitcast(I32), 0.5, None, ALU.mult))
                                link(dve.scalar_tensor_tensor(tF[:, 0:1].bitcast(I32), loF[:, 0:1].bitcast(I32), 0.5,
                                                              c(6), ALU.mult, ALU.add))
                                link(dve.scalar_tensor_tensor(M[:, :], E[:, p, :], tF[:, 0:1], E[:, p, :],
                                                              ALU.is_ge, ALU.mult, accum_out=tF[:, 1:2]))
                                bracket(TT)
                            link(dve.scalar_tensor_tensor(c(6), hiF[:, 0:1], -AIM, TT, ALU.mult, ALU.add))
                            dve.tensor_tensor(c(7), loF[:, 1:2], hiF[:, 1:2], ALU.subtract)
                            link(dve.tensor_tensor(c(6), c(6), hiF[:, 1:2], ALU.subtract))
                            link(dve.tensor_scalar(c(7), c(7), 1e-9, None, ALU.max))
                            link(dve.reciprocal(c(7), c(7)))
                            link(dve.tensor_tensor(c(6), c(6), c(7), ALU.mult))
                            link(dve.tensor_scalar(c(6), c(6), 0.0, 0.98, ALU.max, ALU.min))
                            link(dve.tensor_copy(c(8), hiF[:, 0:1].bitcast(I32)))
                            link(dve.scalar_tensor_tensor(c(7), loF[:, 0:1].bitcast(I32), 1.0, c(8), ALU.mult, ALU.subtract))
                            dve.tensor_tensor(c(9), c(6), c(7), ALU.mult)
                            link(dve.tensor_scalar(c(7), c(7), -512.0, None, ALU.is_ge))
                            link(dve.scalar_tensor_tensor(geo[:, 0:1], c(6), 0.0, c(7), ALU.is_le, ALU.max))
                            link(dve.tensor_tensor(tF[:, 0:1].bitcast(I32), c(8), c(9), ALU.add))
                            link(dve.copy_predicated(tF[:, 0:1], geo[:, 0:1], hiF[:, 0:1]))
                            link(dve.scalar_tensor_tensor(M[:, :], E[:, p, :], tF[:, 0:1], E[:, p, :],
                                                          ALU.is_lt, ALU.mult, accum_out=c(6)))
                            for t in range(T):
                                last = dve.max(CE[:, p, t * G8:(t + 1) * G8], M[:, t * P:(t + 1) * P])
                            link(dve.tensor_tensor(tF[:, 1:2], S[:, p:p + 1], c(6), ALU.subtract))
                            window(CE[:, p, :], WIN, TT, tF[:, 1:2])
                            dve.tensor_tensor(c(6), tF[:, 1:2], TT, ALU.is_ge)
                            link(dve.tensor_tensor(c(7), tF[:, 0:1], st[:, 0:1], ALU.is_ge))
                            link(dve.tensor_tensor(c(7), c(6), c(7), ALU.mult))
                            link(dve.tensor_tensor(c(7), c(7), st[:, 3:4], ALU.mult))
                            dve.tensor_copy(tS[:, 0:1], tF[:, 1:2])
                            dve.memset(tS[:, 1:2], 0.0)
                            link(dve.tensor_scalar(c(8), c(6), -1.0, 1.0, ALU.mult, ALU.add))
                            dve.tensor_scalar(geo[:, :], ones[:, 0:2], c(7), None, ALU.mult)
                            link(dve.tensor_scalar(und[:, :], ones[:, 0:4], c(8), st[:, 3:4], ALU.mult, ALU.mult))
                            link(dve.copy_predicated(st[:, 2:4], geo[:, :], tS[:, :]))
                            link(dve.copy_predicated(st[:, :], und[:, :], new[:, :]))
                            bracket(TT)
                            link(dve.copy_predicated(hiF[:, 0:1], und[:, 0:1], new[:, 0:1]))
                            link(dve.copy_predicated(hiF[:, 1:2], und[:, 0:1], new[:, 2:3]))
                            any_row(st[:, 3:4])
                        fresh()

                    def keep(i, p):
                        TT, v, Fg, Fe = c(0), st[:, 0:1], st[:, 1:2], st[:, 2:3]
                        dve.tensor_tensor(c(2), Fe, Fg, ALU.subtract)
                        dve.tensor_tensor(c(3), TT, Fg, ALU.subtract)
                        link(dve.reciprocal(c(1), v))
                        link(dve.tensor_scalar(sm[:, 2:4], sm[:, 2:4], c(1), None, ALU.mult))
                        dve.tensor_scalar(c(10), c(2), MAGIC, -MAGIC, ALU.add, ALU.add)
                        link(dve.tensor_scalar(c(4), c(3), MAGIC, -MAGIC, ALU.add, ALU.add))
                        dve.tensor_scalar(c(10), c(10), 1.0, None, ALU.max)
                        link(dve.tensor_tensor(c(5), c(3), c(4), ALU.is_gt))
                        link(dve.tensor_tensor(c(4), c(4), c(5), ALU.add))
                        link(dve.scalar_tensor_tensor(c(4), c(4), 1.0, c(10), ALU.max, ALU.min))
                        dve.tensor_tensor(c(5), c(10), c(4), ALU.subtract)
                        link(dve.scalar_tensor_tensor(c(8), c(4), v, Fg, ALU.mult, ALU.add))
                        link(dve.scalar_tensor_tensor(c(8), S[:, p:p + 1], 1e-12, c(8), ALU.mult, ALU.max))
                        link(dve.reciprocal(sinv[:, p:p + 1], c(8)))
                        any_row(c(5))
                        with dve.If(still()):
                            fresh()
                            dve.tensor_tensor(c(5), c(5), v, ALU.mult)
                            link(dve.reciprocal(c(6), c(10)))
                            link(dve.tensor_tensor(c(5), c(5), c(6), ALU.mult))
                            link(dve.tensor_scalar(M[:, :], E[:, p, :], v, c(5), ALU.is_equal, ALU.mult))
                            link(dve.scalar_tensor_tensor(E[:, p, :], E[:, p, :], v, E[:, p, :], ALU.is_ge, ALU.mult))
                            dve.tensor_tensor(E[:, p, :], E[:, p, :], M[:, :], ALU.subtract).then_inc(a_ok, 1)
                        with dve.Else():
                            dve.scalar_tensor_tensor(E[:, p, :], E[:, p, :], v, E[:, p, :],
                                                     ALU.is_ge, ALU.mult).then_inc(a_ok, 1)
                        fresh()

                    def rows(i, p):
                        dve.wait_ge(adj_used, i * 2 + 2)
                        link(dve.tensor_scalar(rinv[:, :], psR[p][:, D:D + 1], 1.0, None, ALU.add))
                        link(dve.reciprocal(rinv[:, :], rinv[:, :]))
                        link(dve.tensor_tensor(xw[:, p, 0, :], psR[p][:, 0:D],
                                               Xf[:, bass.ds(i, 1), 0:D].rearrange("p a d -> p (a d)"), ALU.add))
                        link(dve.tensor_scalar(xw[:, p, 0, :], xw[:, p, 0, :], rinv[:, :], None, ALU.mult))
                        dve.wait_ge(at_used, i * NG + NG)
                        dve.tensor_scalar(xw[:, p, 1, :], psA[:, 0:D], sinv[:, p:p + 1], None, ALU.mult).then_inc(xw_ok, 1)
                        if s == 0:
                            dve.wait_ge(xw_ok, i + 1)
                            dve.tensor_copy(Xf1[:, bass.ds(i, 1), 0:D], xw[:, p, 0:1, :])
                            dve.tensor_copy(Xa1[:, bass.ds(i, 1), :], xw[:, p, 1:2, :])

                    def sums(i, p):
                        if s == 0:
                            prev = X0[:, bass.ds(i, 1), 0:D].rearrange("p a d -> p (a d)")
                        else:
                            dve.wait_ge(hx_in[p], (i - p) * 8 + 16)
                            prev = hx[:, p, :]
                        reach(dve, h_out, i * 16)
                        dve.wait_ge(z_ps, i + 1)
                        if s == 0:
                            dve.tensor_copy(QKn[:, bass.ds(i * P, P)], psM[:, D:D + P])
                        dve.tensor_tensor(hb[:, p, :], psM[:, 0:D], prev, ALU.add).then_inc(h_ok, 1)

                    def turn(k, p):
                        if there(k + 1):
                            largest(k + 1, 1 - p)
                        if there(k):
                            select(k, p)
                            keep(k, p)
                        if there(k - 1):
                            rows(k - 1, 1 - p)
                        if there(k - 2):
                            sums(k - 2, p)

                    dve.memset(zer[:, :], 0.0)
                    dve.memset(ones[:, :], 1.0)
                    dve.memset(fl[:, :], 0.0)
                    link(dve.memset(E[:, :, N:NP], 0.0))
                    run_turns(dve, turn)

        zer = sb("zer", [P, 1])
        geo = sb("geo", [P, 2], I32)
        tS = sb("tS", [P, 2])
        step(0)
        step(1)
        gnn.close()

        xr = sb2("xr", [P, T, D])
        xn = sb2("xn", [P, T, D])
        xnT = sb2("xnT", [P, DK, NP])
        W1e = sb2("W1e", [P, DK, E8, HID])
        W2e = sb2("W2e", [P, HC, E8, D])
        b1T = sb2("b1T", [P, E8, HC])
        b2s = sb2("b2s", [E8, D])
        vec = sb2("vec", [P, 4, D])
        wr = sb2("wr", [P, DK, E8])
        brs = sb2("brs", [P, E8])
        idn = sb2("idn", [P, P])
        stat2 = sb2("stat2", [P, T, 6])
        mv2 = sb2("mv2", [P, T, 2])
        r1 = sb2("r1", [P, T])
        r2 = sb2("r2", [P, T])
        rl = sb2("rl", [P, T, E8])
        top = sb2("top", [P, T, E8])
        wf = sb2("wf", [P, T, E8])
        den = sb2("den", [P, T])
        wT = sb2("wT", [E8, T, P])
        (f_h, f_x, f_w, f_v, f_c, f_sq, f_sqd, f_xn, f_tp, f_te, f_rp, f_rl, f_ex, f_wf, f_wtp, f_wte, f_bp, f_be, i0, i1) = (
            sem(f"f_{k}") for k in range(20))
        with nc.Block() as block:
            @block.sync
            def _(sp):
                sp.dma_start(xn[:, :, :], h_dram).then_inc(f_h, 16)
                sp.dma_start(xr[:, :, :], a["x"].rearrange("(t p) d -> p t d", p=P)).then_inc(f_x, 16)
                sp.dma_start(vec[:, :, :], a["vec"]).then_inc(f_v, 16)
                sp.dma_start(wr[:, :, :], a["Wr"].rearrange("(k p) e -> p k e", p=P)).then_inc(f_v, 16)
                sp.dma_start(brs[:, :], a["br"]).then_inc(f_v, 16)
                sp.dma_start(b2s[:, :], a["b2"]).then_inc(f_v, 16)
                sp.dma_start(b1T[:, :, :], a["b1T"]).then_inc(f_v, 16)
                sp.dma_start(W1e[:, :, :, :], a["W1e"]).then_inc(f_w, 16)
                sp.dma_start(W2e[:, :, :, :], a["W2e"]).then_inc(f_w, 16)
                sp.wait_ge(f_w, 32)

            @block.gpsimd
            def _(pool):
                pool.memset(idn[:, :], 0.0).then_inc(i0, 1)
                pool.wait_ge(i0, 1)
                pool.affine_select(out=idn[:, :], in_=idn[:, :], compare_op=ALU.not_equal, fill=1.0,
                                   base=0, pattern=[[-1, P]], channel_multiplier=1).then_inc(i1, 1)

            @block.vector
            def _(dve):
                n = [0]
                q = [0]

                def link(ins):
                    n[0] += 1
                    ins.then_inc(f_c, 1)
                    dve.wait_ge(f_c, n[0])

                def over_tiles(k):
                    return vec[:, k:k + 1, :].to_broadcast([P, T, D])

                def moments(src):
                    for t in range(T):
                        last = dve.bn_stats(stat2[:, t, :], src[:, t, :])
                    link(last)
                    for t in range(T):
                        last = dve.bn_aggr(mv2[:, t, :], stat2[:, t, :])
                    link(last)

                def rsqrt(r, var):
                    q[0] += 1
                    dve.tensor_scalar(r[:, :], var, EPS, None, ALU.add).then_inc(f_sq, 1)
                    dve.wait_ge(f_sqd, q[0])
                    link(dve.reciprocal(r[:, :], r[:, :]))

                def centre(dst, src, r):
                    for t in range(T):
                        last = dve.tensor_scalar(dst[:, t, :], src[:, t, :], mv2[:, t, 0:1], r[:, t:t + 1],
                                                 ALU.subtract, ALU.mult)
                    link(last)

                dve.wait_ge(f_h, 16)
                moments(xn)
                rsqrt(r1, mv2[:, :, 1])
                centre(xn, xn, r1)
                dve.wait_ge(f_v, 80)
                link(dve.tensor_tensor(xn[:, :, :], xn[:, :, :], over_tiles(0), ALU.mult))
                link(dve.tensor_tensor(xn[:, :, :], xn[:, :, :], over_tiles(1), ALU.add))
                dve.wait_ge(f_x, 16)
                link(dve.tensor_tensor(xr[:, :, :], xr[:, :, :], xn[:, :, :], ALU.add))
                moments(xr)
                rsqrt(r1, mv2[:, :, 1])
                link(dve.tensor_tensor(r2[:, :], r1[:, :], r1[:, :], ALU.mult))
                link(dve.tensor_tensor(r2[:, :], r2[:, :], mv2[:, :, 1], ALU.mult))
                rsqrt(r2, r2[:, :])
                link(dve.tensor_tensor(r1[:, :], r1[:, :], r2[:, :], ALU.mult))
                centre(xn, xr, r1)
                link(dve.tensor_tensor(xn[:, :, :], xn[:, :, :], over_tiles(2), ALU.mult))
                dve.tensor_tensor(xn[:, :, :], xn[:, :, :], over_tiles(3), ALU.add).then_inc(f_xn, 1)
                dve.wait_ge(f_rp, 1)
                link(dve.tensor_tensor(rl[:, :, :], banks[4][:, 0:T * E8].rearrange("p (t e) -> p t e", e=E8),
                                       brs[:, :].rearrange("p (a e) -> p a e", a=1).to_broadcast([P, T, E8]), ALU.add))
                for t in range(T):
                    last = dve.max(top[:, t, :], rl[:, t, :])
                link(last)
                link(dve.tensor_tensor(wf[:, :, :], rl[:, :, :], top[:, :, 0:1].to_broadcast([P, T, E8]), ALU.subtract))
                dve.tensor_tensor(rl[:, :, :], rl[:, :, :], top[:, :, 1:2].to_broadcast([P, T, E8]), ALU.is_ge).then_inc(f_rl, 1)
                dve.wait_ge(f_rl, 1)
                dve.wait_ge(f_ex, 1)
                link(dve.tensor_tensor(wf[:, :, :], wf[:, :, :], rl[:, :, :], ALU.mult))
                link(dve.tensor_reduce(den[:, :], wf[:, :, :], AX.X, ALU.add))
                link(dve.reciprocal(den[:, :], den[:, :]))
                dve.tensor_tensor(wf[:, :, :], wf[:, :, :], den[:, :].rearrange("p (t a) -> p t a", a=1).to_broadcast([P, T, E8]),
                                  ALU.mult).then_inc(f_wf, 1)
                for t in range(T):
                    dve.wait_ge(f_bp, t + 1)
                    dve.tensor_tensor(xr[:, t, :], banks[6 + t % 2][:, 0:D], xr[:, t, :], ALU.add).then_inc(f_be, 1)
                dve.wait_ge(f_be, T)

            @block.scalar
            def _(act):
                for k, r in enumerate((r1, r1, r2)):
                    act.wait_ge(f_sq, k + 1)
                    act.activation(r[:, :], r[:, :], ACT.Sqrt).then_inc(f_sqd, 1)
                for g in range(T // 2):
                    act.wait_ge(f_tp, g + 1)
                    act.copy(xnT[:, :, g * 2 * P:(g + 1) * 2 * P],
                             banks[g % 4][:, :].rearrange("p (k n) -> p k n", k=DK)).then_inc(f_te, 1)
                act.wait_ge(f_rl, 1)
                act.activation(wf[:, :, :], wf[:, :, :], ACT.Exp).then_inc(f_ex, 1)
                for t in range(T):
                    act.wait_ge(f_wtp, t + 1)
                    act.copy(wT[:, t, :], banks[5][0:E8, (t % 4) * P:(t % 4 + 1) * P]).then_inc(f_wte, 1)

            @block.tensor
            def _(pe):
                pe.wait_ge(i1, 1)
                pe.wait_ge(f_xn, 1)
                for g in range(T // 2):
                    if g >= 4:
                        pe.wait_ge(f_te, g - 3)
                    for k in range(DK):
                        for u in range(2):
                            last = pe.transpose(banks[g % 4][:, (k * 2 + u) * P:(k * 2 + u + 1) * P],
                                                xn[:, 2 * g + u, k * P:(k + 1) * P], idn[:, :])
                    last.then_inc(f_tp, 1)
                for t in range(T):
                    pe.wait_ge(f_te, t // 2 + 1)
                    for k in range(DK):
                        last = pe.matmul(banks[4][:, t * E8:(t + 1) * E8], xnT[:, k, t * P:(t + 1) * P], wr[:, k, :],
                                         start=(k == 0), stop=(k == DK - 1))
                last.then_inc(f_rp, 1)
                pe.wait_ge(f_wf, 1)
                for t in range(T):
                    if t >= 4:
                        pe.wait_ge(f_wte, t - 3)
                    pe.transpose(banks[5][0:E8, (t % 4) * P:(t % 4 + 1) * P], wf[:, t, :], idn[:, :]).then_inc(f_wtp, 1)
                    pe.wait_ge(f_wte, t + 1)
                    if t >= 2:
                        pe.wait_ge(f_be, t - 1)
                    pe.matmul(banks[6 + t % 2][:, 0:D], wT[:, t, :], b2s[:, :], start=True, stop=True).then_inc(f_bp, 1)

        G = sb2("G", [P, 2, HC, 2 * P])
        wfs = sb2("wfs", [P, 2, E8])
        acc = sb2("acc", [P, 2, D])
        ob = sb2("ob", [P, 1, 2, D])
        (h_psd, g_ok, y_psd, y_ok, ob_ok, o_done0, xc) = (sem(f"g_{k}") for k in range(7))
        NB = T // 2
        with nc.Block() as block:
            @block.tensor
            def _(pe):
                def up(m, e):
                    k8 = m * E8 + e
                    if not (isinstance(m, int) and e < 2):
                        pe.wait_ge(g_ok, k8 - 1)
                    for c in range(HC):
                        for k in range(DK):
                            last = pe.matmul(banks[2 * (e % 2) + c // 2][:, (c % 2) * 2 * P:(c % 2 + 1) * 2 * P],
                                             W1e[:, k, e, c * P:(c + 1) * P], xnT[:, k, bass.ds(m * 2 * P, 2 * P)],
                                             start=(k == 0), stop=(k == DK - 1))
                    last.then_inc(h_psd, 1)

                def down(m, e):
                    k8 = m * E8 + e
                    pe.wait_ge(g_ok, k8 + 1)
                    if not (isinstance(m, int) and e < 2):
                        pe.wait_ge(y_ok, k8 - 1)
                    for u in range(2):
                        for c in range(HC):
                            last = pe.matmul(banks[4 + e % 2][:, u * D:(u + 1) * D], G[:, e % 2, c, u * P:(u + 1) * P],
                                             W2e[:, c, e, :], start=(c == 0), stop=(c == HC - 1))
                    last.then_inc(y_psd, 1)

                def pair(m):
                    up(m, 0)
                    for e in range(E8):
                        if e + 1 < E8:
                            up(m, e + 1)
                        down(m, e)
                pair(0)
                with pe.Fori(1, NB) as m:
                    pair(m)

            @block.scalar
            def _(act):
                def pair(m):
                    for e in range(E8):
                        k8 = m * E8 + e
                        act.wait_ge(h_psd, k8 + 1)
                        if not (isinstance(m, int) and e < 2):
                            act.wait_ge(y_psd, k8 - 1)
                        for c in range(HC):
                            last = act.activation(G[:, e % 2, c, :], banks[2 * (e % 2) + c // 2][:, (c % 2) * 2 * P:(c % 2 + 1) * 2 * P],
                                                  ACT.Gelu, bias=b1T[:, e, c:c + 1])
                        last.then_inc(g_ok, 1)
                pair(0)
                with act.Fori(1, NB) as m:
                    pair(m)

            @block.vector
            def _(dve):
                ws = wfs

                def pair(m):
                    dve.tensor_copy(ws[:, :, :], wf[:, bass.ds(m * 2, 2), :])
                    dve.tensor_copy(acc[:, :, :], xr[:, bass.ds(m * 2, 2), :]).then_inc(xc, 1)
                    dve.wait_ge(xc, m + 1)
                    for e in range(E8):
                        k8 = m * E8 + e
                        dve.wait_ge(y_psd, k8 + 1)
                        for u in range(2):
                            dst = acc[:, u, :]
                            last = dve.scalar_tensor_tensor(dst, banks[4 + e % 2][:, u * D:(u + 1) * D], ws[:, u, e:e + 1],
                                                            acc[:, u, :], ALU.mult, ALU.add)
                            if e < E8 - 1 and u == 1:
                                last.then_inc(y_ok, 1)
                        if e < E8 - 1:
                            dve.wait_ge(y_ok, k8 + 1)
                    last.then_inc(y_ok, 1)
                    dve.wait_ge(y_ok, m * E8 + E8)
                    if not (isinstance(m, int)):
                        dve.wait_ge(o_done0, m * 16)
                    dve.tensor_copy(ob[:, 0, :, :], acc[:, :, :]).then_inc(ob_ok, 1)
                    dve.wait_ge(ob_ok, m + 1)
                pair(0)
                with dve.Fori(1, NB) as m:
                    pair(m)

            @block.sync
            def _(sp):
                with sp.Fori(0, NB - 1) as m:
                    r0 = sp.snap(m * 2 * P)
                    sp.wait_ge(ob_ok, m + 1)
                    sp.dma_start(out[bass.ds(r0, 2 * P), :].rearrange("(u p) d -> p u d", u=2), ob[:, 0, :, :]).then_inc(o_done0, 16)
                sp.wait_ge(ob_ok, NB)
                sp.dma_start(out[(NB - 1) * 2 * P:(NB - 1) * 2 * P + P, :], ob[:, 0, 0, :]).then_inc(o_done0, 16)
                sp.dma_start(out[(NB - 1) * 2 * P + P:N, :], ob[0:LAST, 0, 1, :]).then_inc(o_done0, 16)
                sp.wait_ge(o_done0, 16 * (NB + 1))


_OUT = ((N, D), "float32")


def kernel(**inputs):
    import numpy as np
    import concourse.bacc as _bacc
    from concourse import mybir as _mybir
    from concourse.bass_utils import run_bass_kernel_spmd as _run

    g = {k: np.asarray(v) for k, v in inputs.items()}
    x = np.concatenate([g["x"], g["x"][N - 1:]])
    adjp = np.zeros((NP, NP), np.float32)
    adjp[:N, :N] = g["adj"]
    lay = {
        "x": x,
        "adjT": adjp.reshape(T, P, T, P).transpose(0, 3, 2, 1),
        "W1": g["L0_gnn_W1"],
        "W2T": g["L0_gnn_W2"].T,
        "W3T": g["L0_gnn_W3"].T,
        "U1T": g["L0_gnn_U1"].transpose(0, 2, 1),
        "U2T": g["L0_gnn_U2"].transpose(0, 2, 1),
        "vec": np.broadcast_to(np.stack([g["L0_gnn_ln_g"], g["L0_gnn_ln_b"], g["L0_ffn_gamma"], g["L0_ffn_beta"]]), (P, 4, D)),
        "Wr": g["L0_ffn_Wr"],
        "br": np.broadcast_to(g["L0_ffn_br"], (P, E8)),
        "W1e": g["L0_ffn_W1"].reshape(E8, DK, P, HID).transpose(2, 1, 0, 3),
        "W2e": g["L0_ffn_W2"].reshape(E8, HC, P, D).transpose(2, 1, 0, 3),
        "b1T": g["L0_ffn_b1"].reshape(E8, HC, P).transpose(2, 0, 1),
        "b2": g["L0_ffn_b2"],
    }
    nc = _bacc.Bacc("TRN2", target_bir_lowering=False, num_devices=1)
    arrays, aps = {}, {}
    for k, v in lay.items():
        v = np.ascontiguousarray(v)
        arrays[f"in_{k}"] = v
        aps[k] = nc.dram_tensor(f"in_{k}", v.shape, _mybir.dt.from_np(v.dtype), kind="ExternalInput").ap()
    o = nc.dram_tensor("out_0", _OUT[0], _mybir.dt.from_np(np.dtype(_OUT[1])), kind="ExternalOutput").ap()
    build(nc, aps, o)
    r = _run(nc, [arrays], core_ids=[0])
    return r.results[0]["out_0"]
```

```python
import concourse.bass as bass
from concourse import mybir
from contextlib import ExitStack

F32 = mybir.dt.float32
I32 = mybir.dt.int32
ALU = mybir.AluOpType
AX = mybir.AxisListType
ACT = mybir.ActivationFunctionType

P = 128
N = 3327
T = -(-N // P)
NP = T * P
LAST = N - (T - 1) * P
D = 256
DK = D // P
DA = 64
TOP_P = 0.9
EPS = 1e-5
CH = 512
CHUNKS = [(c, min(CH, NP - c)) for c in range(0, NP, CH)]
G8 = 8
CW = NP // 16
NC8 = NP // CW * G8
WIN0 = 32
WIN = 48
HALVINGS = 3
AIM = 0.4 * WIN
STEEP = 1e20
TOP = 16.5
LN16 = 2.772588722239781
MAGIC = 12582912.0
HALF = T // 2
PARTS = ((0, 1), (2, 3), (4, 5, 6))
GROUPS = [(g, min(4, T - g)) for g in range(0, T, 4)]
E8 = 8
HID = 512
HC = HID // P


def run_turns(eng, turn):
    for k in range(-2, 2):
        turn(k, k % 2)
    with eng.Fori(0, T // 2 - 2) as m:
        turn(m * 2 + 2, 0)
        turn(m * 2 + 3, 1)
    for k in range(T - 2, T + 2):
        turn(k, k % 2)


def there(i):
    return not isinstance(i, int) or 0 <= i < T


def reach(eng, semaphore, value):
    if not isinstance(value, int) or value > 0:
        eng.wait_ge(semaphore, value)


def build(nc, a, out):
    ctx = ExitStack()
    with ctx:
        gnn = ctx.enter_context(ExitStack())

        def sb(name, shape, dt=F32):
            return gnn.enter_context(nc.sbuf_tensor(name, shape, dt))

        def sb2(name, shape, dt=F32):
            return ctx.enter_context(nc.sbuf_tensor(name, shape, dt))

        def pb(name, cols=512):
            return ctx.enter_context(nc.psum_tensor(name, [P, cols], F32))

        def sem(name):
            return ctx.enter_context(nc.semaphore(name))

        h_dram = nc.dram_tensor("h_dram", (P, T, D), F32, kind="Internal").ap()
        X0 = sb("X0", [P, T, D + 1])
        Xf1 = sb("Xf1", [P, T, D + 1])
        Xa1 = sb("Xa1", [P, T, D])
        QK = sb("QK", [P, NP])
        QKn = sb("QKn", [P, NP])
        ident = sb("ident", [P, P])
        WqkT = sb("WqkT", [P, DK, P])
        W1 = sb("W1", [DA, D])
        W2T = sb("W2T", [DA, DA])
        U1T = sb("U1T", [P, 2, DK, D])
        U2T = sb("U2T", [P, 2, DK, D])
        qw = sb("qw", [DA, 2, P])
        xw = sb("xw", [P, 2, 2, D])
        xT = sb("xT", [P, 4, P])
        hb = sb("hb", [P, 2, D])
        stat = sb("stat", [P, T, 6])
        mv = sb("mv", [P, T, 2])
        rstd = sb("rstd", [P, T])

        banks = [pb(f"bank{i}") for i in range(8)]
        psL = banks[0:2]
        psT = banks[2:4]
        psR = banks[4:6]
        psA = banks[6]
        psM = banks[7]

        x_in, w_in, st_ok, sq_ok, id0, id1 = (sem(n) for n in ("x_in", "w_in", "st_ok", "sq_ok", "id0", "id1"))
        wq_ps, wq_ok, xn_ok, xt_ps, xt_ok, qk_ps, qk_ok, c1 = (sem(n) for n in (
            "wq_ps", "wq_ok", "xn_ok", "xt_ps", "xt_ok", "qk_ps", "qk_ok", "c1"))
        xall = Xf1[:, :, 0:D]
        with nc.Block() as block:
            @block.sync
            def _(sp):
                sp.dma_start(xall, a["x"].rearrange("(t p) d -> p t d", p=P)).then_inc(x_in, 16)
                sp.dma_start(W1[:, :], a["W1"]).then_inc(w_in, 16)
                sp.dma_start(W2T[:, :], a["W2T"]).then_inc(w_in, 16)
                sp.dma_start(WqkT[:, :, 0:DA], a["W3T"].rearrange("(k p) n -> p k n", p=P)).then_inc(w_in, 16)
                sp.dma_start(U1T[:, :, :, :], a["U1T"].rearrange("s (k p) n -> p s k n", p=P)).then_inc(w_in, 16)
                sp.dma_start(U2T[:, :, :, :], a["U2T"].rearrange("s (k p) n -> p s k n", p=P)).then_inc(w_in, 16)
                sp.wait_ge(w_in, 80)

            @block.gpsimd
            def _(pool):
                pool.memset(ident[:, :], 0.0).then_inc(id0, 1)
                pool.wait_ge(id0, 1)
                pool.affine_select(out=ident[:, :], in_=ident[:, :], compare_op=ALU.not_equal, fill=1.0,
                                   base=0, pattern=[[-1, P]], channel_multiplier=1).then_inc(id1, 1)

            @block.vector
            def _(dve):
                dve.memset(X0[:, :, D:D + 1], 1.0)
                dve.wait_ge(x_in, 16)
                for t in range(T):
                    last = dve.bn_stats(stat[:, t, :], xall[:, t, :])
                last.then_inc(c1, 1)
                dve.wait_ge(c1, 1)
                for t in range(T):
                    last = dve.bn_aggr(mv[:, t, :], stat[:, t, :])
                last.then_inc(c1, 1)
                dve.wait_ge(c1, 2)
                dve.tensor_scalar(rstd[:, :], mv[:, :, 1], EPS, None, ALU.add).then_inc(st_ok, 1)
                dve.wait_ge(sq_ok, 1)
                dve.reciprocal(rstd[:, :], rstd[:, :]).then_inc(c1, 1)
                dve.wait_ge(wq_ps, 1)
                dve.tensor_copy(WqkT[:, :, DA:P], psM[:, 0:P].rearrange("p (k n) -> p k n", k=DK)).then_inc(wq_ok, 1)
                dve.wait_ge(c1, 3)
                for t in range(T):
                    dve.tensor_scalar(X0[:, t, 0:D], xall[:, t, :], mv[:, t, 0:1], rstd[:, t:t + 1],
                                      ALU.subtract, ALU.mult).then_inc(xn_ok, 1)
                dve.wait_ge(xn_ok, T)
                dve.memset(Xf1[:, :, D:D + 1], 1.0)

            @block.scalar
            def _(act):
                act.wait_ge(st_ok, 1)
                act.activation(rstd[:, :], rstd[:, :], ACT.Sqrt).then_inc(sq_ok, 1)

                def take_turned(t):
                    act.wait_ge(xt_ps, t + 1)
                    if t >= 2:
                        act.wait_ge(qk_ps, t - 1)
                    act.copy(xT[:, t % 2 * DK:(t % 2 + 1) * DK, :],
                             psT[t % 2][:, 0:D].rearrange("p (k n) -> p k n", k=DK)).then_inc(xt_ok, 1)

                take_turned(0)
                for t in range(T):
                    if t + 1 < T:
                        take_turned(t + 1)
                    act.wait_ge(qk_ps, t + 1)
                    act.copy(QK[:, t * P:(t + 1) * P], psL[t % 2][:, 0:P]).then_inc(qk_ok, 1)

            @block.tensor
            def _(pe):
                pe.wait_ge(w_in, 80)
                for k in range(DK):
                    last = pe.matmul(psM[:, k * DA:(k + 1) * DA], W1[:, k * P:(k + 1) * P], W2T[:, :],
                                     start=True, stop=True)
                last.then_inc(wq_ps, 1)
                pe.wait_ge(id1, 1)
                pe.wait_ge(wq_ok, 1)

                def turned(t):
                    pe.wait_ge(xn_ok, t + 1)
                    if t >= 2:
                        pe.wait_ge(xt_ok, t - 1)
                    for k in range(DK):
                        last = pe.transpose(psT[t % 2][:, k * P:(k + 1) * P], X0[:, t, k * P:(k + 1) * P], ident[:, :])
                    last.then_inc(xt_ps, 1)

                turned(0)
                for t in range(T):
                    if t + 1 < T:
                        turned(t + 1)
                    pe.wait_ge(xt_ok, t + 1)
                    if t >= 2:
                        pe.wait_ge(qk_ok, t - 1)
                    for k in range(DK):
                        last = pe.matmul(psL[t % 2][:, 0:P], WqkT[:, k, :], xT[:, t % 2 * DK + k, :],
                                         start=(k == 0), stop=(k == DK - 1))
                    last.then_inc(qk_ps, 1)

        L = sb("L", [P, NP])
        E = sb("E", [P, 2, NP])
        M = sb("M", [P, NP])
        adj = sb("adj", [P, 2, HALF, P])
        AT = sb("AT", [P, 2, 4, P])
        CL = sb("CL", [P, 2, NC8])
        CE = sb("CE", [P, 2, NC8])
        U = sb("U", [P, WIN])
        cum = sb("cum", [P, WIN])
        wv = sb("wv", [P, WIN])
        ones = sb("ones", [P, WIN])
        nm = sb("nm", [P, 2])
        S = sb("S", [P, 2])
        st = sb("st", [P, 4])
        new = sb("new", [P, 4])
        und = sb("und", [P, 4], I32)
        hiF = sb("hiF", [P, 2])
        tF = sb("tF", [P, 2])
        loF = sb("loF", [P, 2])
        sm = sb("sm", [P, 16])
        gei = sb("gei", [P, 2], I32)
        fl = sb("fl", [P, 32])
        flT = sb("flT", [P, 32])
        fr = sb("fr", [P, 1])
        fg = sb("fg", [1, 4])
        open_i = sb("open_i", [1, 1], I32)
        sinv = sb("sinv", [P, 2])
        rinv = sb("rinv", [P, 1])
        hx = sb("hx", [P, 2, D])

        def step(s):
            Xf, Xa = (X0, X0) if s == 0 else (Xf1, Xa1)
            qk = QK if s == 0 else QKn
            adj_in = [sem(f"adj_in{h}_{s}") for h in range(2)]
            hx_in = [sem(f"hx_in{h}_{s}") for h in range(2)]
            (adj_used, qw_ok, lg_ps, lg_ev, cl_ok, e_ok, a_ok, t_ps,
             t_ev, at_used, xw_ok, xt_ps, xt_ok, z_ps, h_ok, h_out, ce_ok, ch, g_ok, pch, probe_ok, probed, probed0, s_ok, last_ok, lasted) = (
                sem(f"{name}_{s}") for name in (
                    "adj_used", "qw_ok", "lg_ps", "lg_ev", "cl_ok", "e_ok", "a_ok", "t_ps",
                    "t_ev", "at_used", "xw_ok", "xt_ps", "xt_ok", "z_ps", "h_ok", "h_out", "ce_ok", "ch", "g_ok", "pch", "probe_ok", "probed", "probed0", "s_ok", "last_ok", "lasted"))
            NCH = len(CHUNKS)
            NG = len(GROUPS)
            with nc.Block() as block:
                @block.sync
                def _(sp):
                    for h in range(2):
                        sp.dma_start(adj[:, h, :, :], a["adjT"][0, :, h * HALF:(h + 1) * HALF, :]).then_inc(adj_in[h], 16)
                    with sp.Fori(1, T) as i:
                        for h in range(2):
                            free = sp.snap(i * 2 - 1 + h)
                            src = a["adjT"][bass.ds(i, 1), :, h * HALF:(h + 1) * HALF, :]
                            sp.wait_ge(adj_used, free)
                            sp.dma_start(adj[:, h, :, :], src.rearrange("a p j n -> p (a j) n")).then_inc(adj_in[h], 16)

                @block.gpsimd
                def _(pool):
                    n = [0]

                    def link(ins):
                        n[0] += 1
                        ins.then_inc(pch, 1)
                        pool.wait_ge(pch, n[0])

                    q = lambda k: pm[:, k:k + 1]

                    def guess(i, p):
                        TG, LT, GE, W = q(0), q(1), q(2), q(7)
                        pool.sem_clear(pch)
                        n[0] = 0
                        pool.wait_ge(s_ok, 1)
                        pool.sem_clear(s_ok)
                        pool.tensor_scalar(TG, SG[:, 0:1], TOP_P, None, ALU.mult)
                        pool.tensor_scalar(loG[:, 1:2], SG[:, 0:1], 0.95, None, ALU.mult)
                        pool.memset(tb[:, 0:1], TOP)
                        pool.memset(hiG[:, 1:2], 0.0)
                        link(pool.tensor_scalar(q(3), SG[:, 0:1], (1 - TOP_P) * 0.9 / NP, None, ALU.mult))
                        pool.tensor_copy(hiG[:, 0:1], tb[:, 0:1].bitcast(I32))
                        link(pool.tensor_copy(loG[:, 0:1], q(3).bitcast(I32)))
                        link(pool.tensor_tensor(q(3), hiG[:, 0:1], loG[:, 0:1], ALU.add))
                        pool.tensor_scalar(tG[:, 0:1], q(3), 0.5, None, ALU.mult)
                        link(pool.tensor_scalar(tb[:, 0:1].bitcast(I32), q(3), 0.5, None, ALU.mult))
                        pool.tensor_scalar(ntb[:, 0:1], tb[:, 0:1], -1.0, None, ALU.mult).then_inc(probe_ok, 1)
                        link(pool.tensor_tensor(W, loG[:, 0:1], hiG[:, 0:1], ALU.subtract))
                        for r in range(HALVINGS):
                            mass = tG[:, 1:2]
                            if r < HALVINGS - 1:
                                link(pool.tensor_scalar(W, W, 0.5, None, ALU.mult))
                                link(pool.tensor_scalar(q(6), W, -0.5, tG[:, 0:1], ALU.mult, ALU.add))
                                pool.wait_ge(probed0, 1)
                                pool.sem_clear(probed0)
                                pool.wait_ge(probed, 1)
                                pool.sem_clear(probed)
                                link(pool.tensor_scalar(q(4), pr[:, 1:2], float(N), 0.5, ALU.add, ALU.mult))
                                link(pool.tensor_scalar(mass, q(4), tb[:, 0:1], pr[:, 0:1], ALU.mult, ALU.add))
                                link(pool.tensor_scalar(q(5), mass, TG, W, ALU.is_lt, ALU.mult))
                                link(pool.tensor_scalar(tb[:, 0:1].bitcast(I32), q(5), q(6), None, ALU.add))
                                pool.tensor_scalar(ntb[:, 0:1], tb[:, 0:1], -1.0, None,
                                                   ALU.mult).then_inc(probe_ok if r < HALVINGS - 2 else last_ok, 1)
                            else:
                                pool.wait_ge(lasted, 1)
                                pool.sem_clear(lasted)
                                link(pool.tensor_copy(mass, m3[:, 0:1]))
                            pool.tensor_scalar(LT, mass, TG, None, ALU.is_lt)
                            pool.tensor_scalar(GE, mass, TG, None, ALU.is_ge)
                            pool.tensor_tensor(dG[:, 0:2], tG[:, :], loG[:, :], ALU.subtract)
                            link(pool.tensor_tensor(dG[:, 2:4], tG[:, :], hiG[:, :], ALU.subtract))
                            pool.tensor_scalar(dG[:, 0:2], dG[:, 0:2], GE, None, ALU.mult)
                            link(pool.tensor_scalar(dG[:, 2:4], dG[:, 2:4], LT, None, ALU.mult))
                            pool.tensor_tensor(loG[:, :], loG[:, :], dG[:, 0:2], ALU.add)
                            link(pool.tensor_tensor(hiG[:, :], hiG[:, :], dG[:, 2:4], ALU.add))
                            if r < HALVINGS - 1:
                                link(pool.tensor_tensor(tG[:, 0:1], q(5), q(6), ALU.add))
                        link(pool.tensor_copy(tb[:, 0:1].bitcast(I32), hiG[:, 0:1]))
                        pool.tensor_tensor(q(5), loG[:, 1:2], hiG[:, 1:2], ALU.subtract)
                        pool.tensor_tensor(q(6), loG[:, 0:1], hiG[:, 0:1], ALU.subtract)
                        pool.tensor_tensor(q(4), TG, hiG[:, 1:2], ALU.subtract)
                        link(pool.tensor_scalar(q(3), tb[:, 0:1], AIM, None, ALU.mult))
                        pool.memset(q(8), -1.0)
                        pool.tensor_scalar(q(5), q(5), 1e-9, None, ALU.max)
                        link(pool.tensor_tensor(q(4), q(4), q(3), ALU.subtract))
                        link(pool.tensor_tensor(q(5), q(5), q(8), ALU.pow))
                        link(pool.tensor_tensor(q(4), q(4), q(5), ALU.mult))
                        link(pool.tensor_scalar(q(4), q(4), 0.0, 0.98, ALU.max, ALU.min))
                        link(pool.tensor_tensor(q(4), q(4), q(6), ALU.mult))
                        link(pool.tensor_tensor(q(4), q(4), hiG[:, 0:1], ALU.add))
                        pool.tensor_copy(aimed[:, p:p + 1].bitcast(I32), q(4)).then_inc(g_ok, 1)

                    def put(i, p):
                        dst = h_dram[:, bass.ds(i, 1), :]
                        pool.wait_ge(h_ok, i + 1)
                        pool.dma_start(dst, hb[:, p:p + 1, :]).then_inc(h_out, 16)
                    if s == 0:
                        with pool.Fori(0, T // 2) as m:
                            put(m * 2, 0)
                            put(m * 2 + 1, 1)
                    else:
                        for p in range(2):
                            pool.dma_start(hx[:, p:p + 1, :], h_dram[:, p:p + 1, :]).then_inc(hx_in[p], 16)
                        guess(0, 0)
                        guess(1, 1)
                        guess(2, 0)
                        with pool.Fori(0, T // 2 - 2) as m:
                            for p in range(2):
                                guess(m * 2 + 3 + p, 1 - p)
                                put(m * 2 + p, p)
                                pool.dma_start(hx[:, p:p + 1, :], h_dram[:, bass.ds(m * 2 + 2 + p, 1), :]).then_inc(hx_in[p], 16)
                        guess(T - 1, 1)
                        for i in range(T - 4, T):
                            put(i, i % 2)
                            if i + 2 < T:
                                pool.dma_start(hx[:, i % 2:i % 2 + 1, :], h_dram[:, i + 2:i + 3, :]).then_inc(hx_in[i % 2], 16)
                    pool.wait_ge(h_out, 16 * T)

                @block.tensor
                def _(pe):
                    def turned(i, p, g):
                        g0, n = GROUPS[g]
                        reach(pe, t_ev, i * NG + g - 1)
                        for y in range(n):
                            last = pe.transpose(psT[(p * NG + g) % 2][:, y * P:(y + 1) * P],
                                                E[:, p, (g0 + y) * P:(g0 + y + 1) * P], ident[:, :])
                        last.then_inc(t_ps, 1)

                    def attend(i, p, between):
                        pe.wait_ge(a_ok, i + 1)
                        turned(i, p, 0)
                        for g, (g0, n) in enumerate(GROUPS):
                            if g + 1 < NG:
                                turned(i, p, g + 1)
                            if g == 1:
                                between()
                            pe.wait_ge(t_ev, i * NG + g + 1)
                            if g == 0:
                                reach(pe, xw_ok, i)
                            for y in range(n):
                                jt = g0 + y
                                last = pe.matmul(psA[:, 0:D], AT[:, (p * NG + g) % 2, y, :], Xa[:, jt, 0:D],
                                                 start=(jt == 0), stop=(jt == T - 1))
                            last.then_inc(at_used, 1)

                    def post_turn(i, p):
                        pe.wait_ge(xw_ok, i + 1)
                        reach(pe, h_ok, i)
                        for y in range(4):
                            last = pe.transpose(psM[:, y * P:(y + 1) * P], xw[:, p, y // 2, (y % 2) * P:(y % 2 + 1) * P],
                                                ident[:, :])
                        last.then_inc(xt_ps, 1)

                    def post_products(i):
                        pe.wait_ge(xt_ok, i + 1)
                        for y in range(4):
                            w = U1T if y < 2 else U2T
                            last = pe.matmul(psM[:, 0:D], xT[:, y, :], w[:, s, y % 2, :], start=(y == 0), stop=(y == 3))
                        if s == 0:
                            for k in range(DK):
                                last = pe.matmul(psM[:, D:D + P], WqkT[:, k, :], xT[:, 2 + k, :], start=(k == 0), stop=(k == 1))
                        last.then_inc(z_ps, 1)

                    def diffuse(i, p, h):
                        if h == 0:
                            reach(pe, xw_ok, i - 1)
                        pe.wait_ge(adj_in[h], i * 16 + 16)
                        for j in range(HALF):
                            jt = h * HALF + j
                            last = pe.matmul(psR[p][:, 0:D + 1], adj[:, h, j, :], Xf[:, jt, :],
                                             start=(jt == 0), stop=(jt == T - 1))
                        last.then_inc(adj_used, 1)

                    def logits(i, p, part):
                        if part == 0:
                            pe.wait_ge(qw_ok, i + 1)
                        for c in PARTS[part]:
                            c0, w = CHUNKS[c]
                            reach(pe, lg_ev, i * NCH + c - 1)
                            pe.matmul(psL[(p * NCH + c) % 2][:, 0:w], qw[:, p, :], qk[0:DA, c0:c0 + w],
                                      start=True, stop=True).then_inc(lg_ps, 1)

                    def turn(k, p):
                        if there(k - 2):
                            post_turn(k - 2, p)
                        if there(k - 1):
                            attend(k - 1, 1 - p, lambda: post_products(k - 2) if there(k - 2) else None)
                        elif there(k - 2):
                            post_products(k - 2)
                        for part in range(3):
                            if there(k + 2):
                                logits(k + 2, p, part)
                            if there(k) and part < 2:
                                diffuse(k, p, part)

                    run_turns(pe, turn)

                @block.scalar
                def _(act):
                    def candidates(i, p):
                        act.wait_ge(cl_ok, i + 1)
                        act.activation(CE[:, p, :], CL[:, p, :], ACT.Exp, bias=nm[:, p:p + 1]).then_inc(ce_ok, 1)

                    def exponentials(i, p):
                        act.wait_ge(cl_ok, i + 1)
                        reach(act, t_ps, (i - 1) * NG)
                        act.activation(E[:, p, 0:N], L[:, 0:N], ACT.Exp, bias=nm[:, p:p + 1],
                                       accum_out=S[:, p:p + 1]).then_inc(e_ok, 1)

                    def probe(i, p, between):
                        act.wait_ge(e_ok, i + 1)
                        reach(act, g_ok, i)
                        act.copy(SG[:, 0:1], S[:, p:p + 1]).then_inc(s_ok, 1)
                        for r in range(HALVINGS - 1):
                            between(r + 1)
                            act.wait_ge(probe_ok, i * (HALVINGS - 1) + r + 1)
                            act.activation(QK[:, 0:N], E[:, p, 0:N], ACT.Relu, bias=ntb[:, 0:1],
                                           accum_out=pr[:, 0:1]).then_inc(probed0, 1)
                            act.activation(X0[:, :, :].rearrange("p t d -> p (t d)")[:, 0:N], E[:, p, 0:N], ACT.Sign, bias=ntb[:, 0:1],
                                           accum_out=pr[:, 1:2]).then_inc(probed, 1)

                    def queries(i, p):
                        act.copy(qw[:, p, :], qk[DA:P, bass.ds(i * P, P)]).then_inc(qw_ok, 1)

                    def take_logits(i, p, part):
                        if part == 0 and there(i - 1):
                            act.wait_ge(e_ok, i)
                        for c in PARTS[part]:
                            c0, w = CHUNKS[c]
                            act.wait_ge(lg_ps, i * NCH + c + 1)
                            act.copy(L[:, c0:c0 + w], psL[(p * NCH + c) % 2][:, 0:w]).then_inc(lg_ev, 1)

                    def take_turned(i, p, g):
                        g0, n = GROUPS[g]
                        gb = (p * NG + g) % 2
                        act.wait_ge(t_ps, i * NG + g + 1)
                        reach(act, at_used, i * NG + g - 1)
                        act.activation(AT[:, gb, 0:n, :], psT[gb][:, 0:n * P].rearrange("p (y n) -> p y n", y=n),
                                       ACT.Relu).then_inc(t_ev, 1)

                    def take_rows(i):
                        act.wait_ge(xt_ps, i + 1)
                        reach(act, z_ps, i)
                        act.copy(xT[:, :, :], psM[:, :].rearrange("p (y n) -> p y n", y=4)).then_inc(xt_ok, 1)

                    def turn(k, p):
                        if there(k + 2):
                            queries(k + 2, p)
                        if there(k - 2):
                            take_rows(k - 2)
                        if there(k - 1):
                            for g in range(NG):
                                take_turned(k - 1, 1 - p, g)
                        if there(k + 1):
                            if s == 0:
                                candidates(k + 1, 1 - p)
                            exponentials(k + 1, 1 - p)
                        part_of = lambda part: take_logits(k + 2, p, part) if there(k + 2) else None
                        if s == 1 and there(k + 1):
                            probe(k + 1, 1 - p, lambda r: part_of(r - 1))
                            part_of(2)
                        else:
                            for part in range(3):
                                part_of(part)

                    run_turns(act, turn)

                @block.vector
                def _(dve):
                    n = [0]

                    def link(ins):
                        n[0] += 1
                        ins.then_inc(ch, 1)
                        dve.wait_ge(ch, n[0])

                    def fresh():
                        dve.sem_clear(ch)
                        n[0] = 0

                    c = lambda k: sm[:, k:k + 1]

                    def largest(i, p):
                        fresh()
                        dve.wait_ge(lg_ev, (i + 1) * NCH)
                        link(dve.memset(c(15), 0.0))
                        if s == 0:
                            for t in range(NP // CW):
                                last = dve.max(CL[:, p, t * G8:(t + 1) * G8], L[:, t * CW:min((t + 1) * CW, N)])
                            link(last)
                            link(dve.tensor_reduce(c(15), CL[:, p, :], AX.X, ALU.max))
                        else:
                            link(dve.tensor_reduce(c(15), L[:, 0:N], AX.X, ALU.max))
                        dve.tensor_scalar(nm[:, p:p + 1], c(15), -1.0, LN16, ALU.mult, ALU.add).then_inc(cl_ok, 1)

                    def window(C, W, TT, Fh):
                        link(dve.tensor_reduce(c(1), C[:, G8 - 1:NC8:G8], AX.X, ALU.max))
                        for r in range(W // G8):
                            link(dve.max(U[:, r * G8:(r + 1) * G8], C))
                            if r < W // G8 - 1:
                                link(dve.match_replace(C, U[:, r * G8:(r + 1) * G8], C, 0.0))
                        link(dve.tensor_tensor_scan(cum[:, 0:W], ones[:, 0:W], U[:, 0:W], Fh, ALU.mult, ALU.add))
                        link(dve.scalar_tensor_tensor(wv[:, 0:W], cum[:, 0:W], TT, U[:, 0:W], ALU.is_ge, ALU.mult))
                        dve.tensor_reduce(c(2), wv[:, 0:W], AX.X, ALU.max)
                        link(dve.tensor_tensor(c(3), U[:, W - 1:W], c(1), ALU.max))
                        dve.tensor_tensor(new[:, 3:4], c(2), c(3), ALU.is_le)
                        link(dve.tensor_tensor(new[:, 0:1], c(2), c(3), ALU.max))
                        link(dve.scalar_tensor_tensor(wv[:, 0:W], U[:, 0:W], new[:, 0:1], U[:, 0:W], ALU.is_gt, ALU.mult,
                                                      accum_out=c(4)))
                        link(dve.scalar_tensor_tensor(wv[:, 0:W], U[:, 0:W], new[:, 0:1], U[:, 0:W], ALU.is_ge, ALU.mult,
                                                      accum_out=c(5)))
                        link(dve.tensor_scalar(new[:, 1:3], sm[:, 4:6], Fh, None, ALU.add))

                    def any_row(x):
                        link(dve.tensor_scalar(fl[:, 0:1], x, 0.0, None, ALU.is_gt))
                        link(dve.transpose(flT[:, :], fl[:, :]))
                        link(dve.tensor_reduce(fr[:, :], flT[:, :], AX.X, ALU.max))
                        for q in range(4):
                            last = dve.tensor_copy(fg[0:1, q:q + 1], fr[32 * q:32 * q + 1, :])
                        link(last)
                        link(dve.tensor_reduce(open_i[:, :], fg[:, :], AX.X, ALU.max))

                    def still():
                        return dve.value_load(open_i[0:1, 0:1])

                    def bracket(TT):
                        dve.tensor_tensor(gei[:, 0:1], tF[:, 1:2], TT, ALU.is_lt)
                        dve.tensor_tensor(gei[:, 1:2], tF[:, 1:2], TT, ALU.is_lt)
                        dve.tensor_tensor(geo[:, 0:1], tF[:, 1:2], TT, ALU.is_ge)
                        link(dve.tensor_tensor(geo[:, 1:2], tF[:, 1:2], TT, ALU.is_ge))
                        dve.copy_predicated(hiF[:, :], gei[:, :], tF[:, :])
                        link(dve.copy_predicated(loF[:, :], geo[:, :], tF[:, :]))

                    def below(p, TT):
                        link(dve.scalar_tensor_tensor(M[:, :], E[:, p, :], tF[:, 0:1], E[:, p, :],
                                                      ALU.is_lt, ALU.mult, accum_out=c(6)))
                        for t in range(NP // CW):
                            last = dve.max(CE[:, p, t * G8:(t + 1) * G8], M[:, t * CW:(t + 1) * CW])
                        link(dve.tensor_tensor(tF[:, 1:2], S[:, p:p + 1], c(6), ALU.subtract))
                        window(CE[:, p, :], WIN, TT, tF[:, 1:2])
                        dve.tensor_tensor(c(6), tF[:, 1:2], TT, ALU.is_ge)
                        link(dve.tensor_tensor(c(7), tF[:, 0:1], st[:, 0:1], ALU.is_ge))
                        link(dve.tensor_tensor(c(7), c(6), c(7), ALU.mult))
                        link(dve.tensor_tensor(c(7), c(7), st[:, 3:4], ALU.mult))
                        dve.tensor_copy(tS[:, 0:1], tF[:, 1:2])
                        dve.memset(tS[:, 1:2], 0.0)
                        link(dve.tensor_scalar(c(8), c(6), -1.0, 1.0, ALU.mult, ALU.add))
                        dve.tensor_scalar(geo[:, :], ones[:, 0:2], c(7), None, ALU.mult)
                        link(dve.tensor_scalar(und[:, :], ones[:, 0:4], c(8), st[:, 3:4], ALU.mult, ALU.mult))
                        link(dve.copy_predicated(st[:, 2:4], geo[:, :], tS[:, :]))
                        link(dve.copy_predicated(st[:, :], und[:, :], new[:, :]))
                        bracket(TT)
                        link(dve.copy_predicated(hiF[:, 0:1], und[:, 0:1], new[:, 0:1]))
                        link(dve.copy_predicated(hiF[:, 1:2], und[:, 0:1], new[:, 2:3]))

                    def select(i, p):
                        TT = c(0)
                        fresh()
                        dve.wait_ge(e_ok, i + 1)
                        dve.tensor_scalar(loF[:, 0:1], S[:, p:p + 1], (1 - TOP_P) * 0.9 / NP, None, ALU.mult)
                        dve.tensor_scalar(loF[:, 1:2], S[:, p:p + 1], 0.95, None, ALU.mult)
                        link(dve.tensor_scalar(TT, S[:, p:p + 1], TOP_P, None, ALU.mult))
                        if s == 0:
                            window(CE[:, p, :], WIN0, TT, zer[:, 0:1])
                            dve.tensor_copy(hiF[:, 0:1], new[:, 0:1])
                            dve.tensor_copy(hiF[:, 1:2], new[:, 2:3])
                            link(dve.tensor_copy(st[:, :], new[:, :]))
                        else:
                            dve.wait_ge(g_ok, i + 1)
                            dve.tensor_copy(tF[:, 0:1], aimed[:, p:p + 1])
                            dve.memset(hiF[:, 0:1], TOP)
                            dve.memset(hiF[:, 1:2], 0.0)
                            dve.memset(st[:, 0:1], TOP)
                            dve.memset(st[:, 1:3], 0.0)
                            link(dve.memset(st[:, 3:4], 1.0))
                            below(p, TT)
                        any_row(st[:, 3:4])

                        with dve.While(still):
                            fresh()
                            for _ in range(HALVINGS):
                                link(dve.tensor_scalar(c(6), hiF[:, 0:1].bitcast(I32), 0.5, None, ALU.mult))
                                link(dve.scalar_tensor_tensor(tF[:, 0:1].bitcast(I32), loF[:, 0:1].bitcast(I32), 0.5,
                                                              c(6), ALU.mult, ALU.add))
                                link(dve.scalar_tensor_tensor(M[:, :], E[:, p, :], tF[:, 0:1], E[:, p, :],
                                                              ALU.is_ge, ALU.mult, accum_out=tF[:, 1:2]))
                                bracket(TT)
                            link(dve.scalar_tensor_tensor(c(6), hiF[:, 0:1], -AIM, TT, ALU.mult, ALU.add))
                            dve.tensor_tensor(c(7), loF[:, 1:2], hiF[:, 1:2], ALU.subtract)
                            link(dve.tensor_tensor(c(6), c(6), hiF[:, 1:2], ALU.subtract))
                            link(dve.tensor_scalar(c(7), c(7), 1e-9, None, ALU.max))
                            link(dve.reciprocal(c(7), c(7)))
                            link(dve.tensor_tensor(c(6), c(6), c(7), ALU.mult))
                            link(dve.tensor_scalar(c(6), c(6), 0.0, 0.98, ALU.max, ALU.min))
                            link(dve.tensor_copy(c(8), hiF[:, 0:1].bitcast(I32)))
                            link(dve.scalar_tensor_tensor(c(7), loF[:, 0:1].bitcast(I32), 1.0, c(8), ALU.mult, ALU.subtract))
                            dve.tensor_tensor(c(9), c(6), c(7), ALU.mult)
                            link(dve.tensor_scalar(c(7), c(7), -512.0, None, ALU.is_ge))
                            link(dve.scalar_tensor_tensor(geo[:, 0:1], c(6), 0.0, c(7), ALU.is_le, ALU.max))
                            link(dve.tensor_tensor(tF[:, 0:1].bitcast(I32), c(8), c(9), ALU.add))
                            link(dve.copy_predicated(tF[:, 0:1], geo[:, 0:1], hiF[:, 0:1]))
                            below(p, TT)
                            any_row(st[:, 3:4])
                        fresh()

                    def keep(i, p):
                        TT, v, Fg, Fe = c(0), st[:, 0:1], st[:, 1:2], st[:, 2:3]
                        dve.tensor_tensor(c(2), Fe, Fg, ALU.subtract)
                        dve.tensor_tensor(c(3), TT, Fg, ALU.subtract)
                        link(dve.reciprocal(c(1), v))
                        link(dve.tensor_scalar(sm[:, 2:4], sm[:, 2:4], c(1), None, ALU.mult))
                        dve.tensor_scalar(c(10), c(2), MAGIC, -MAGIC, ALU.add, ALU.add)
                        link(dve.tensor_scalar(c(4), c(3), MAGIC, -MAGIC, ALU.add, ALU.add))
                        dve.tensor_scalar(c(10), c(10), 1.0, None, ALU.max)
                        link(dve.tensor_tensor(c(5), c(3), c(4), ALU.is_gt))
                        link(dve.tensor_tensor(c(4), c(4), c(5), ALU.add))
                        link(dve.scalar_tensor_tensor(c(4), c(4), 1.0, c(10), ALU.max, ALU.min))
                        dve.reciprocal(c(6), c(10))
                        link(dve.scalar_tensor_tensor(c(8), c(4), v, Fg, ALU.mult, ALU.add))
                        dve.tensor_scalar(c(7), c(4), v, c(6), ALU.mult, ALU.mult)
                        link(dve.scalar_tensor_tensor(c(8), S[:, p:p + 1], 1e-12, c(8), ALU.mult, ALU.max))
                        dve.reciprocal(sinv[:, p:p + 1], c(8))
                        link(dve.tensor_scalar(M[:, 0:N], E[:, p, 0:N], v, STEEP, ALU.subtract, ALU.mult))
                        dve.scalar_tensor_tensor(E[:, p, 0:N], M[:, 0:N], c(7), E[:, p, 0:N],
                                                 ALU.add, ALU.min).then_inc(a_ok, 1)

                    def rows(i, p):
                        dve.wait_ge(adj_used, i * 2 + 2)
                        link(dve.tensor_scalar(rinv[:, :], psR[p][:, D:D + 1], 1.0, None, ALU.add))
                        link(dve.reciprocal(rinv[:, :], rinv[:, :]))
                        link(dve.tensor_tensor(xw[:, p, 0, :], psR[p][:, 0:D],
                                               Xf[:, bass.ds(i, 1), 0:D].rearrange("p a d -> p (a d)"), ALU.add))
                        link(dve.tensor_scalar(xw[:, p, 0, :], xw[:, p, 0, :], rinv[:, :], None, ALU.mult))
                        dve.wait_ge(at_used, i * NG + NG)
                        dve.tensor_scalar(xw[:, p, 1, :], psA[:, 0:D], sinv[:, p:p + 1], None, ALU.mult).then_inc(xw_ok, 1)
                        if s == 0:
                            dve.wait_ge(xw_ok, i + 1)
                            dve.tensor_copy(Xf1[:, bass.ds(i, 1), 0:D], xw[:, p, 0:1, :])
                            dve.tensor_copy(Xa1[:, bass.ds(i, 1), :], xw[:, p, 1:2, :])

                    def sums(i, p):
                        if s == 0:
                            prev = X0[:, bass.ds(i, 1), 0:D].rearrange("p a d -> p (a d)")
                        else:
                            dve.wait_ge(hx_in[p], (i - p) * 8 + 16)
                            prev = hx[:, p, :]
                        reach(dve, h_out, i * 16)
                        dve.wait_ge(z_ps, i + 1)
                        if s == 0:
                            dve.tensor_copy(QKn[:, bass.ds(i * P, P)], psM[:, D:D + P])
                        dve.tensor_tensor(hb[:, p, :], psM[:, 0:D], prev, ALU.add).then_inc(h_ok, 1)

                    def last_probe(i, p):
                        dve.wait_ge(last_ok, i + 1)
                        link(dve.memset(c(14), 0.0))
                        dve.scalar_tensor_tensor(M[:, :], E[:, p, :], tb[:, 0:1], E[:, p, :],
                                                 ALU.is_ge, ALU.mult, accum_out=m3[:, 0:1]).then_inc(lasted, 1)

                    def turn(k, p):
                        if there(k + 1):
                            largest(k + 1, 1 - p)
                        if there(k):
                            select(k, p)
                        if there(k - 2):
                            sums(k - 2, p)
                        if there(k):
                            keep(k, p)
                        if there(k - 1):
                            rows(k - 1, 1 - p)
                        if s == 1 and there(k + 1):
                            last_probe(k + 1, 1 - p)

                    dve.memset(zer[:, :], 0.0)
                    dve.memset(ones[:, :], 1.0)
                    dve.memset(fl[:, :], 0.0)
                    link(dve.memset(E[:, :, N:NP], 0.0))
                    run_turns(dve, turn)

        zer = sb("zer", [P, 1])
        geo = sb("geo", [P, 2], I32)
        tS = sb("tS", [P, 2])
        pm = sb("pm", [P, 10])
        tb = sb("tb", [P, 1])
        loG = sb("loG", [P, 2])
        hiG = sb("hiG", [P, 2])
        tG = sb("tG", [P, 2])
        dG = sb("dG", [P, 4])
        SG = sb("SG", [P, 1])
        ntb = sb("ntb", [P, 1])
        m3 = sb("m3", [P, 1])
        pr = sb("pr", [P, 2])
        aimed = sb("aimed", [P, 2])
        step(0)
        step(1)
        gnn.close()

        xr = sb2("xr", [P, T, D])
        xn = sb2("xn", [P, T, D])
        xnT = sb2("xnT", [P, DK, NP])
        W1e = sb2("W1e", [P, DK, E8, HID])
        W2e = sb2("W2e", [P, HC, E8, D])
        b1T = sb2("b1T", [P, E8, HC])
        b2s = sb2("b2s", [E8, D])
        vec = sb2("vec", [P, 4, D])
        wr = sb2("wr", [P, DK, E8])
        brs = sb2("brs", [P, E8])
        idn = sb2("idn", [P, P])
        stat2 = sb2("stat2", [P, T, 6])
        mv2 = sb2("mv2", [P, T, 2])
        r1 = sb2("r1", [P, T])
        r2 = sb2("r2", [P, T])
        rl = sb2("rl", [P, T, E8])
        top = sb2("top", [P, T, E8])
        wf = sb2("wf", [P, T, E8])
        den = sb2("den", [P, T])
        wT = sb2("wT", [E8, T, P])
        (f_h, f_x, f_w, f_v, f_c, f_sq, f_sqd, f_xn, f_tp, f_te, f_rp, f_rl, f_ex, f_wf, f_wtp, f_wte, f_bp, f_be, i0, i1) = (
            sem(f"f_{k}") for k in range(20))
        with nc.Block() as block:
            @block.sync
            def _(sp):
                sp.dma_start(xn[:, :, :], h_dram).then_inc(f_h, 16)
                sp.dma_start(xr[:, :, :], a["x"].rearrange("(t p) d -> p t d", p=P)).then_inc(f_x, 16)
                sp.dma_start(vec[:, :, :], a["vec"]).then_inc(f_v, 16)
                sp.dma_start(wr[:, :, :], a["Wr"].rearrange("(k p) e -> p k e", p=P)).then_inc(f_v, 16)
                sp.dma_start(brs[:, :], a["br"]).then_inc(f_v, 16)
                sp.dma_start(b2s[:, :], a["b2"]).then_inc(f_v, 16)
                sp.dma_start(b1T[:, :, :], a["b1T"]).then_inc(f_v, 16)
                sp.dma_start(W1e[:, :, :, :], a["W1e"]).then_inc(f_w, 16)
                sp.dma_start(W2e[:, :, :, :], a["W2e"]).then_inc(f_w, 16)
                sp.wait_ge(f_w, 32)

            @block.gpsimd
            def _(pool):
                pool.memset(idn[:, :], 0.0).then_inc(i0, 1)
                pool.wait_ge(i0, 1)
                pool.affine_select(out=idn[:, :], in_=idn[:, :], compare_op=ALU.not_equal, fill=1.0,
                                   base=0, pattern=[[-1, P]], channel_multiplier=1).then_inc(i1, 1)

            @block.vector
            def _(dve):
                n = [0]
                q = [0]

                def link(ins):
                    n[0] += 1
                    ins.then_inc(f_c, 1)
                    dve.wait_ge(f_c, n[0])

                def over_tiles(k):
                    return vec[:, k:k + 1, :].to_broadcast([P, T, D])

                def moments(src):
                    for t in range(T):
                        last = dve.bn_stats(stat2[:, t, :], src[:, t, :])
                    link(last)
                    for t in range(T):
                        last = dve.bn_aggr(mv2[:, t, :], stat2[:, t, :])
                    link(last)

                def rsqrt(r, var):
                    q[0] += 1
                    dve.tensor_scalar(r[:, :], var, EPS, None, ALU.add).then_inc(f_sq, 1)
                    dve.wait_ge(f_sqd, q[0])
                    link(dve.reciprocal(r[:, :], r[:, :]))

                def centre(dst, src, r):
                    for t in range(T):
                        last = dve.tensor_scalar(dst[:, t, :], src[:, t, :], mv2[:, t, 0:1], r[:, t:t + 1],
                                                 ALU.subtract, ALU.mult)
                    link(last)

                dve.wait_ge(f_h, 16)
                moments(xn)
                rsqrt(r1, mv2[:, :, 1])
                centre(xn, xn, r1)
                dve.wait_ge(f_v, 80)
                link(dve.tensor_tensor(xn[:, :, :], xn[:, :, :], over_tiles(0), ALU.mult))
                link(dve.tensor_tensor(xn[:, :, :], xn[:, :, :], over_tiles(1), ALU.add))
                dve.wait_ge(f_x, 16)
                link(dve.tensor_tensor(xr[:, :, :], xr[:, :, :], xn[:, :, :], ALU.add))
                moments(xr)
                rsqrt(r1, mv2[:, :, 1])
                link(dve.tensor_tensor(r2[:, :], r1[:, :], r1[:, :], ALU.mult))
                link(dve.tensor_tensor(r2[:, :], r2[:, :], mv2[:, :, 1], ALU.mult))
                rsqrt(r2, r2[:, :])
                link(dve.tensor_tensor(r1[:, :], r1[:, :], r2[:, :], ALU.mult))
                centre(xn, xr, r1)
                link(dve.tensor_tensor(xn[:, :, :], xn[:, :, :], over_tiles(2), ALU.mult))
                dve.tensor_tensor(xn[:, :, :], xn[:, :, :], over_tiles(3), ALU.add).then_inc(f_xn, 1)
                dve.wait_ge(f_rp, 1)
                link(dve.tensor_tensor(rl[:, :, :], banks[4][:, 0:T * E8].rearrange("p (t e) -> p t e", e=E8),
                                       brs[:, :].rearrange("p (a e) -> p a e", a=1).to_broadcast([P, T, E8]), ALU.add))
                for t in range(T):
                    last = dve.max(top[:, t, :], rl[:, t, :])
                link(last)
                link(dve.tensor_tensor(wf[:, :, :], rl[:, :, :], top[:, :, 0:1].to_broadcast([P, T, E8]), ALU.subtract))
                dve.tensor_tensor(rl[:, :, :], rl[:, :, :], top[:, :, 1:2].to_broadcast([P, T, E8]), ALU.is_ge).then_inc(f_rl, 1)
                dve.wait_ge(f_rl, 1)
                dve.wait_ge(f_ex, 1)
                link(dve.tensor_tensor(wf[:, :, :], wf[:, :, :], rl[:, :, :], ALU.mult))
                link(dve.tensor_reduce(den[:, :], wf[:, :, :], AX.X, ALU.add))
                link(dve.reciprocal(den[:, :], den[:, :]))
                dve.tensor_tensor(wf[:, :, :], wf[:, :, :], den[:, :].rearrange("p (t a) -> p t a", a=1).to_broadcast([P, T, E8]),
                                  ALU.mult).then_inc(f_wf, 1)
                for t in range(T):
                    dve.wait_ge(f_bp, t + 1)
                    dve.tensor_tensor(xr[:, t, :], banks[6 + t % 2][:, 0:D], xr[:, t, :], ALU.add).then_inc(f_be, 1)
                dve.wait_ge(f_be, T)

            @block.scalar
            def _(act):
                for k, r in enumerate((r1, r1, r2)):
                    act.wait_ge(f_sq, k + 1)
                    act.activation(r[:, :], r[:, :], ACT.Sqrt).then_inc(f_sqd, 1)
                for g in range(T // 2):
                    act.wait_ge(f_tp, g + 1)
                    act.copy(xnT[:, :, g * 2 * P:(g + 1) * 2 * P],
                             banks[g % 4][:, :].rearrange("p (k n) -> p k n", k=DK)).then_inc(f_te, 1)
                act.wait_ge(f_rl, 1)
                act.activation(wf[:, :, :], wf[:, :, :], ACT.Exp).then_inc(f_ex, 1)
                for t in range(T):
                    act.wait_ge(f_wtp, t + 1)
                    act.copy(wT[:, t, :], banks[2 + t % 4][0:E8, 0:P]).then_inc(f_wte, 1)

            @block.tensor
            def _(pe):
                def weighted_b2(t):
                    pe.wait_ge(f_wte, t + 1)
                    if t >= 2:
                        pe.wait_ge(f_be, t - 1)
                    pe.matmul(banks[6 + t % 2][:, 0:D], wT[:, t, :], b2s[:, :], start=True, stop=True).then_inc(f_bp, 1)

                pe.wait_ge(i1, 1)
                pe.wait_ge(f_xn, 1)
                for g in range(T // 2):
                    if g >= 4:
                        pe.wait_ge(f_te, g - 3)
                    for k in range(DK):
                        for u in range(2):
                            last = pe.transpose(banks[g % 4][:, (k * 2 + u) * P:(k * 2 + u + 1) * P],
                                                xn[:, 2 * g + u, k * P:(k + 1) * P], idn[:, :])
                    last.then_inc(f_tp, 1)
                for t in range(T):
                    pe.wait_ge(f_te, t // 2 + 1)
                    for k in range(DK):
                        last = pe.matmul(banks[4][:, t * E8:(t + 1) * E8], xnT[:, k, t * P:(t + 1) * P], wr[:, k, :],
                                         start=(k == 0), stop=(k == DK - 1))
                last.then_inc(f_rp, 1)
                pe.wait_ge(f_wf, 1)
                for t in range(T):
                    if t >= 4:
                        pe.wait_ge(f_wte, t - 3)
                    pe.transpose(banks[2 + t % 4][0:E8, 0:P], wf[:, t, :], idn[:, :]).then_inc(f_wtp, 1)
                    if t >= 2:
                        weighted_b2(t - 2)
                weighted_b2(T - 2)
                weighted_b2(T - 1)

        G = sb2("G", [P, 2, HC, 2 * P])
        wfs = sb2("wfs", [P, 2, E8])
        acc = sb2("acc", [P, 2, D])
        ob = sb2("ob", [P, 1, 2, D])
        (h_psd, g_ok, y_psd, y_ok, ob_ok, o_done0, xc) = (sem(f"g_{k}") for k in range(7))
        NB = T // 2
        with nc.Block() as block:
            @block.tensor
            def _(pe):
                def up(m, e):
                    k8 = m * E8 + e
                    if not (isinstance(m, int) and e < 2):
                        pe.wait_ge(g_ok, k8 - 1)
                    for c in range(HC):
                        for k in range(DK):
                            last = pe.matmul(banks[2 * (e % 2) + c // 2][:, (c % 2) * 2 * P:(c % 2 + 1) * 2 * P],
                                             W1e[:, k, e, c * P:(c + 1) * P], xnT[:, k, bass.ds(m * 2 * P, 2 * P)],
                                             start=(k == 0), stop=(k == DK - 1))
                    last.then_inc(h_psd, 1)

                def down(m, e):
                    k8 = m * E8 + e
                    pe.wait_ge(g_ok, k8 + 1)
                    if not (isinstance(m, int) and e < 2):
                        pe.wait_ge(y_ok, k8 - 1)
                    for u in range(2):
                        for c in range(HC):
                            last = pe.matmul(banks[4 + e % 2][:, u * D:(u + 1) * D], G[:, e % 2, c, u * P:(u + 1) * P],
                                             W2e[:, c, e, :], start=(c == 0), stop=(c == HC - 1))
                    last.then_inc(y_psd, 1)

                def pair(m):
                    up(m, 0)
                    for e in range(E8):
                        if e + 1 < E8:
                            up(m, e + 1)
                        down(m, e)
                pair(0)
                with pe.Fori(1, NB) as m:
                    pair(m)

            @block.scalar
            def _(act):
                def pair(m):
                    for e in range(E8):
                        k8 = m * E8 + e
                        act.wait_ge(h_psd, k8 + 1)
                        if not (isinstance(m, int) and e < 2):
                            act.wait_ge(y_psd, k8 - 1)
                        for c in range(HC):
                            last = act.activation(G[:, e % 2, c, :], banks[2 * (e % 2) + c // 2][:, (c % 2) * 2 * P:(c % 2 + 1) * 2 * P],
                                                  ACT.Gelu, bias=b1T[:, e, c:c + 1])
                        last.then_inc(g_ok, 1)
                pair(0)
                with act.Fori(1, NB) as m:
                    pair(m)

            @block.vector
            def _(dve):
                ws = wfs

                def pair(m):
                    dve.tensor_copy(ws[:, :, :], wf[:, bass.ds(m * 2, 2), :])
                    dve.tensor_copy(acc[:, :, :], xr[:, bass.ds(m * 2, 2), :]).then_inc(xc, 1)
                    dve.wait_ge(xc, m + 1)
                    for e in range(E8):
                        k8 = m * E8 + e
                        dve.wait_ge(y_psd, k8 + 1)
                        for u in range(2):
                            dst = acc[:, u, :]
                            last = dve.scalar_tensor_tensor(dst, banks[4 + e % 2][:, u * D:(u + 1) * D], ws[:, u, e:e + 1],
                                                            acc[:, u, :], ALU.mult, ALU.add)
                            if e < E8 - 1 and u == 1:
                                last.then_inc(y_ok, 1)
                        if e < E8 - 1:
                            dve.wait_ge(y_ok, k8 + 1)
                    last.then_inc(y_ok, 1)
                    dve.wait_ge(y_ok, m * E8 + E8)
                    if not (isinstance(m, int)):
                        dve.wait_ge(o_done0, m * 16)
                    dve.tensor_copy(ob[:, 0, :, :], acc[:, :, :]).then_inc(ob_ok, 1)
                    dve.wait_ge(ob_ok, m + 1)
                pair(0)
                with dve.Fori(1, NB) as m:
                    pair(m)

            @block.sync
            def _(sp):
                with sp.Fori(0, NB - 1) as m:
                    r0 = sp.snap(m * 2 * P)
                    sp.wait_ge(ob_ok, m + 1)
                    sp.dma_start(out[bass.ds(r0, 2 * P), :].rearrange("(u p) d -> p u d", u=2), ob[:, 0, :, :]).then_inc(o_done0, 16)
                sp.wait_ge(ob_ok, NB)
                sp.dma_start(out[(NB - 1) * 2 * P:(NB - 1) * 2 * P + P, :], ob[:, 0, 0, :]).then_inc(o_done0, 16)
                sp.dma_start(out[(NB - 1) * 2 * P + P:N, :], ob[0:LAST, 0, 1, :]).then_inc(o_done0, 16)
                sp.wait_ge(o_done0, 16 * (NB + 1))


_OUT = ((N, D), "float32")


def kernel(**inputs):
    import numpy as np
    import concourse.bacc as _bacc
    from concourse import mybir as _mybir
    from concourse.bass_utils import run_bass_kernel_spmd as _run

    g = {k: np.asarray(v) for k, v in inputs.items()}
    x = np.concatenate([g["x"], g["x"][N - 1:]])
    adjp = np.zeros((NP, NP), np.float32)
    adjp[:N, :N] = g["adj"]
    lay = {
        "x": x,
        "adjT": adjp.reshape(T, P, T, P).transpose(0, 3, 2, 1),
        "W1": g["L0_gnn_W1"],
        "W2T": g["L0_gnn_W2"].T,
        "W3T": g["L0_gnn_W3"].T,
        "U1T": g["L0_gnn_U1"].transpose(0, 2, 1),
        "U2T": g["L0_gnn_U2"].transpose(0, 2, 1),
        "vec": np.broadcast_to(np.stack([g["L0_gnn_ln_g"], g["L0_gnn_ln_b"], g["L0_ffn_gamma"], g["L0_ffn_beta"]]), (P, 4, D)),
        "Wr": g["L0_ffn_Wr"],
        "br": np.broadcast_to(g["L0_ffn_br"], (P, E8)),
        "W1e": g["L0_ffn_W1"].reshape(E8, DK, P, HID).transpose(2, 1, 0, 3),
        "W2e": g["L0_ffn_W2"].reshape(E8, HC, P, D).transpose(2, 1, 0, 3),
        "b1T": g["L0_ffn_b1"].reshape(E8, HC, P).transpose(2, 0, 1),
        "b2": g["L0_ffn_b2"],
    }
    nc = _bacc.Bacc("TRN2", target_bir_lowering=False, num_devices=1)
    arrays, aps = {}, {}
    for k, v in lay.items():
        v = np.ascontiguousarray(v)
        arrays[f"in_{k}"] = v
        aps[k] = nc.dram_tensor(f"in_{k}", v.shape, _mybir.dt.from_np(v.dtype), kind="ExternalInput").ap()
    o = nc.dram_tensor("out_0", _OUT[0], _mybir.dt.from_np(np.dtype(_OUT[1])), kind="ExternalOutput").ap()
    build(nc, aps, o)
    r = _run(nc, [arrays], core_ids=[0])
    return r.results[0]["out_0"]
```
